# Optimizing a Trainium2 kernel written in Bass

```python
import numpy as np
import jax
import jax.numpy as jnp

def _softmax(x, axis=-1):
    return jax.nn.softmax(x, axis=axis)

def _gelu(x):
    return jax.nn.gelu(x, approximate=True)

def _silu(x):
    return jax.nn.silu(x)

def _sigmoid(x):
    return jax.nn.sigmoid(x)

def _layernorm(x, axis=-1, eps=1e-05):
    m = jnp.mean(x, axis=axis, keepdims=True)
    v = jnp.var(x, axis=axis, keepdims=True)
    return (x - m) / jnp.sqrt(v + eps)

def _scatter_add(tgt, idx, src, axis=0):
    return tgt.at[idx].add(src)

def _segment_sum(src, seg, n):
    return jax.ops.segment_sum(src, seg, n)
kernel_name = 'mk_audio_tower_d1_tok_audfeat512_r4_99af03'

def setup_inputs(seed: int=0):
    np.random.seed(seed)
    _w = jnp.asarray

    def _rec_inputs():
        import jax
        import jax.numpy as jnp
        _rk = jax.random.key(seed)
        x = -0.000392918 + 0.999932 * jax.random.normal(jax.random.fold_in(_rk, 1), (8, 256, 128), jnp.float32)
        return x
    x = _rec_inputs()

    def _L0_tok_setup():
        import jax, jax.numpy as jnp
        import numpy as np
        B, T, D, H = (8, 1024, 128, 128)

        def _linear_params(key, d_in, d_out):
            k1, k2 = jax.random.split(key)
            bound = 1.0 / np.sqrt(d_in)
            W = jax.random.uniform(k1, (d_in, d_out), jnp.float32, -bound, bound)
            b = jax.random.uniform(k2, (d_out,), jnp.float32, -bound, bound)
            return (W, b)

        def _log_g(z):
            return jnp.where(z >= 0, jnp.log(jax.nn.relu(z) + 0.5), -jax.nn.softplus(-z))
        key = jax.random.key(seed)
        kx, kf, ki, kh = jax.random.split(key, 4)
        x = jax.random.normal(kx, (B, T, D), dtype=jnp.float32)
        Wf, bf = _linear_params(kf, D, H)
        Wi, bi = _linear_params(ki, D, H)
        Wh, bh = _linear_params(kh, D, H)
        return {'x': x, 'Wf': Wf, 'bf': bf, 'Wi': Wi, 'bi': bi, 'Wh': Wh, 'bh': bh}
    _L0_tok_all = _L0_tok_setup()
    _L0_tok_in = {k: v for k, v in _L0_tok_all.items() if k in ('Wf', 'bf', 'Wi', 'bi', 'Wh', 'bh')}
    del _L0_tok_all

    def _L0_attn_setup():
        import jax, jax.numpy as jnp
        import numpy as np
        NUM_HEADS = 8
        key = jax.random.key(seed)
        k1, k2, k3 = jax.random.split(key, 3)
        B, N, C = (4, 512, 128)
        x = jax.random.normal(k1, (B, N, C), dtype=jnp.float32)
        q_w = jax.random.normal(k2, (C, C), dtype=jnp.float32) * 0.02
        kv_w = jax.random.normal(k3, (2 * C, C), dtype=jnp.float32) * 0.02
        return {'x': x, 'q_w': q_w, 'kv_w': kv_w}
    _L0_attn_all = _L0_attn_setup()
    _L0_attn_in = {k: v for k, v in _L0_attn_all.items() if k in ('q_w', 'kv_w')}
    del _L0_attn_all

    def _L0_ffn_setup():
        import jax, jax.numpy as jnp
        import numpy as np
        B, S, D = (4, 512, 128)
        I = 96
        E = 16
        K = 2

        def _inv_softplus(v):
            return float(np.log(np.expm1(v)))

        def swiglu5(h, alpha, gate_scale, up_shift, gate_clamp_raw, up_clamp_raw):
            gate_clamp = jax.nn.softplus(gate_clamp_raw)
            up_clamp = jax.nn.softplus(up_clamp_raw)
            g = jnp.clip(h[..., ::2], -gate_clamp, gate_clamp)
            u = jnp.clip(h[..., 1::2], -up_clamp, up_clamp)
            return g * jax.nn.sigmoid(g * alpha) * gate_scale * (u + up_shift)
        key = jax.random.key(seed)
        ks = jax.random.split(key, 10)
        std = 0.02
        raw = _inv_softplus(7.0)
        act = jnp.array([1.702, 1.0, 1.0, raw, raw], dtype=jnp.float32)
        return {'x': jax.random.normal(ks[0], (B, S, D), dtype=jnp.float32), 'gate_w': jax.random.normal(ks[1], (D, E), dtype=jnp.float32) * 0.01, 'gate_b': jnp.zeros((E,), dtype=jnp.float32), 'shared_w1': jax.random.normal(ks[2], (D, 2 * I), dtype=jnp.float32) * std, 'shared_b1': jnp.zeros((2 * I,), dtype=jnp.float32), 'shared_w2': jax.random.normal(ks[3], (I, D), dtype=jnp.float32) * std, 'shared_b2': jnp.zeros((D,), dtype=jnp.float32), 'shared_act': act, 'expert_w1': jax.random.normal(ks[4], (E, D, 2 * I), dtype=jnp.float32) * std, 'expert_b1': jnp.zeros((E, 2 * I), dtype=jnp.float32), 'expert_w2': jax.random.normal(ks[5], (E, I, D), dtype=jnp.float32) * std, 'expert_b2': jnp.zeros((E, D), dtype=jnp.float32), 'expert_act': jnp.tile(act[None, :], (E, 1))}
    _L0_ffn_all = _L0_ffn_setup()
    _L0_ffn_in = {k: v for k, v in _L0_ffn_all.items() if k in ('gate_w', 'gate_b', 'shared_w1', 'shared_b1', 'shared_w2', 'shared_b2', 'shared_act', 'expert_w1', 'expert_b1', 'expert_w2', 'expert_b2', 'expert_act')}
    del _L0_ffn_all
    return {'x': x, 'L0_tok_Wf': _L0_tok_in['Wf'], 'L0_tok_bf': _L0_tok_in['bf'], 'L0_tok_Wi': _L0_tok_in['Wi'], 'L0_tok_bi': _L0_tok_in['bi'], 'L0_tok_Wh': _L0_tok_in['Wh'], 'L0_tok_bh': _L0_tok_in['bh'], 'L0_attn_q_w': _L0_attn_in['q_w'], 'L0_attn_kv_w': _L0_attn_in['kv_w'], 'L0_ffn_gate_w': _L0_ffn_in['gate_w'], 'L0_ffn_gate_b': _L0_ffn_in['gate_b'], 'L0_ffn_shared_w1': _L0_ffn_in['shared_w1'], 'L0_ffn_shared_b1': _L0_ffn_in['shared_b1'], 'L0_ffn_shared_w2': _L0_ffn_in['shared_w2'], 'L0_ffn_shared_b2': _L0_ffn_in['shared_b2'], 'L0_ffn_shared_act': _L0_ffn_in['shared_act'], 'L0_ffn_expert_w1': _L0_ffn_in['expert_w1'], 'L0_ffn_expert_b1': _L0_ffn_in['expert_b1'], 'L0_ffn_expert_w2': _L0_ffn_in['expert_w2'], 'L0_ffn_expert_b2': _L0_ffn_in['expert_b2'], 'L0_ffn_expert_act': _L0_ffn_in['expert_act']}

def reference(x, L0_tok_Wf, L0_tok_bf, L0_tok_Wi, L0_tok_bi, L0_tok_Wh, L0_tok_bh, L0_attn_q_w, L0_attn_kv_w, L0_ffn_gate_w, L0_ffn_gate_b, L0_ffn_shared_w1, L0_ffn_shared_b1, L0_ffn_shared_w2, L0_ffn_shared_b2, L0_ffn_shared_act, L0_ffn_expert_w1, L0_ffn_expert_b1, L0_ffn_expert_w2, L0_ffn_expert_b2, L0_ffn_expert_act):
    import jax
    import jax.numpy as jnp

    def _L0_tok_ref(x, Wf, bf, Wi, bi, Wh, bh):
        import jax, jax.numpy as jnp
        import numpy as np
        B, T, D, H = (8, 1024, 128, 128)

        def _linear_params(key, d_in, d_out):
            k1, k2 = jax.random.split(key)
            bound = 1.0 / np.sqrt(d_in)
            W = jax.random.uniform(k1, (d_in, d_out), jnp.float32, -bound, bound)
            b = jax.random.uniform(k2, (d_out,), jnp.float32, -bound, bound)
            return (W, b)

        def _log_g(z):
            return jnp.where(z >= 0, jnp.log(jax.nn.relu(z) + 0.5), -jax.nn.softplus(-z))
        b, t, h = (x.shape[0], x.shape[1], Wf.shape[1])
        zf = x @ Wf + bf
        zi = x @ Wi + bi
        zh = x @ Wh + bh
        diff = jax.nn.softplus(-zf) - jax.nn.softplus(-zi)
        log_f = -jax.nn.softplus(diff)
        log_i = -jax.nn.softplus(-diff)
        log_h0 = jnp.full((b, 1, h), jnp.log(jnp.float32(0.5)), dtype=x.dtype)
        log_tilde_h = _log_g(zh)
        log_val = jnp.concatenate([log_h0, log_i + log_tilde_h], axis=1)
        a_star = jnp.concatenate([jnp.zeros((b, 1, h), dtype=x.dtype), log_f], axis=1)
        log_h = a_star + jax.lax.cumlogsumexp(log_val - a_star, axis=1)
        return jnp.exp(log_h)

    def _L0_attn_ref(x, q_w, kv_w):
        import jax, jax.numpy as jnp
        import numpy as np
        NUM_HEADS = 8
        B, N, C = x.shape
        H = NUM_HEADS
        D = C // H
        halfB = B // 2
        q = (x @ q_w.T).reshape(B, N, H, D)
        kv = (x @ kv_w.T).reshape(B, N, 2, H, D)
        k, v = (kv[:, :, 0], kv[:, :, 1])
        k = jnp.concatenate([k[halfB:], k[:halfB]], axis=0)
        v = jnp.concatenate([v[halfB:], v[:halfB]], axis=0)
        scores = jnp.einsum('bnhd,bmhd->bhnm', q, k) / jnp.sqrt(jnp.float32(C))
        prob = jax.nn.softmax(scores, axis=-1)
        out = jnp.einsum('bhnm,bmhd->bndh', prob, v).reshape(B, N, C)
        return out

    def _L0_ffn_ref(x, gate_w, gate_b, shared_w1, shared_b1, shared_w2, shared_b2, shared_act, expert_w1, expert_b1, expert_w2, expert_b2, expert_act):
        import jax, jax.numpy as jnp
        import numpy as np
        B, S, D = (4, 512, 128)
        I = 96
        E = 16
        K = 2

        def _inv_softplus(v):
            return float(np.log(np.expm1(v)))

        def swiglu5(h, alpha, gate_scale, up_shift, gate_clamp_raw, up_clamp_raw):
            gate_clamp = jax.nn.softplus(gate_clamp_raw)
            up_clamp = jax.nn.softplus(up_clamp_raw)
            g = jnp.clip(h[..., ::2], -gate_clamp, gate_clamp)
            u = jnp.clip(h[..., 1::2], -up_clamp, up_clamp)
            return g * jax.nn.sigmoid(g * alpha) * gate_scale * (u + up_shift)
        shape = x.shape
        xf = x.reshape(-1, shape[-1])
        h = xf @ shared_w1 + shared_b1
        t = swiglu5(h, shared_act[0], shared_act[1], shared_act[2], shared_act[3], shared_act[4])
        z = t @ shared_w2 + shared_b2
        gate_logits = xf @ gate_w + gate_b
        gate_probs = jax.nn.softmax(gate_logits, -1)
        w, idx = jax.lax.top_k(gate_probs, K)
        w = w / jnp.sum(w, axis=-1, keepdims=True)
        cw = jnp.sum(jax.nn.one_hot(idx, E, dtype=xf.dtype) * w[..., None], axis=1)
        he = jnp.einsum('nd,edh->enh', xf, expert_w1) + expert_b1[:, None, :]
        a = expert_act
        te = swiglu5(he, a[:, 0, None, None], a[:, 1, None, None], a[:, 2, None, None], a[:, 3, None, None], a[:, 4, None, None])
        oe = jnp.einsum('enh,ehd->end', te, expert_w2) + expert_b2[:, None, :]
        y = jnp.einsum('ne,end->nd', cw, oe)
        return (y + z).reshape(shape)
    h = _L0_tok_ref(x, L0_tok_Wf, L0_tok_bf, L0_tok_Wi, L0_tok_bi, L0_tok_Wh, L0_tok_bh)
    h = h + _L0_attn_ref(_layernorm(h, axis=-1), L0_attn_q_w, L0_attn_kv_w)
    h = h + _L0_ffn_ref(_layernorm(h, axis=-1), L0_ffn_gate_w, L0_ffn_gate_b, L0_ffn_shared_w1, L0_ffn_shared_b1, L0_ffn_shared_w2, L0_ffn_shared_b2, L0_ffn_shared_act, L0_ffn_expert_w1, L0_ffn_expert_b1, L0_ffn_expert_w2, L0_ffn_expert_b2, L0_ffn_expert_act)
    return h

_drawn_inputs = setup_inputs


def setup_inputs(seed=0):
    import zlib

    import numpy as np

    out = dict(_drawn_inputs(seed))
    spreads = {'L0_ffn_gate_b': (0.0, 0.8),
     'L0_ffn_shared_b1': (0.0, 0.8),
     'L0_ffn_shared_b2': (0.0, 0.8),
     'L0_ffn_expert_b1': (0.0, 0.8),
     'L0_ffn_expert_b2': (0.0, 0.8)}
    factors = {'L0_tok_bf': 3.504,
     'L0_tok_bi': 4.863,
     'L0_attn_q_w': 8.0,
     'L0_attn_kv_w': 8.0,
     'L0_ffn_gate_w': 8.0,
     'L0_ffn_shared_w1': 8.0,
     'L0_ffn_shared_w2': 8.0,
     'L0_ffn_shared_act': 8.0,
     'L0_ffn_expert_w1': 8.0,
     'L0_ffn_expert_w2': 8.0,
     'L0_ffn_expert_act': 8.0}
    for name, (base, spread) in spreads.items():
        noise = np.random.default_rng([zlib.crc32(name.encode()), seed]).standard_normal(out[name].shape)
        drawn = base * np.exp(spread * noise) if base else spread * noise
        out[name] = jnp.asarray(drawn.astype(out[name].dtype))
    for name, factor in factors.items():
        out[name] = (out[name] * factor).astype(out[name].dtype)
    return out
```

```python
from contextlib import ExitStack

import numpy as np
import concourse.bass as bass
from concourse import mybir

F32 = mybir.dt.float32
F32R = mybir.dt.float32r
ALU = mybir.AluOpType
ACT = mybir.ActivationFunctionType
AX_X = mybir.AxisListType.X

P = 128
B, T, D = 8, 256, 128
N = T + 1
W = N + 1
UNITS = B // 2
H, DH = 8, 16
PAIRS = H // 2
E, I = 16, 96
NE = E + 1
NF = -(-NE * I // P)
CH = 5
SCORE_SCALE = float(D) ** -0.5
EPS = 1e-5
SET_EXP_LN = 6
SET_EXP_TANH = 0
LOOP = True
STEP = 3
LAST = slice(2 * W - 2 - STEP * (P - 1), 2 * W - 1, STEP)
ROWS = ((N - 1 - LAST.start) // STEP, P - 1)

CONSTS = {}
_at = 0
for _name, _n in (("wtok", 3 * P), ("btok", 3), ("cmat", P), ("omat", P), ("wq", P), ("wk", P), ("wv", P),
                  ("ident", P), ("ones32", 64), ("mask8", P), ("maskp", 2), ("gate_w", E), ("gate_b", E),
                  ("rank", E), ("b2", P), ("par", 7 * NF)):
    CONSTS[_name] = (_at, _at + _n)
    _at += _n
NCONST = _at

MAXES = [("max", s, c, t) for s in range(2) for c in range(2) for t in range(PAIRS)]


def scores(s, c):
    return [("st", s, c, t) for t in range(PAIRS)]


USES = (["zfi", "zh", ("cent", 1), ("var", 1), "q", "k", "v"] + MAXES + [("mlast", 0), ("mlast", 1), ("plast", 0)]
        + scores(0, 0) + scores(0, 1) + [("plast", 1)] + scores(1, 0) + scores(1, 1)
        + [("cent", 2), ("var", 2), "gate", "cwt"] + [(x, c) for c in range(NF) for x in ("g", "u", "cw")] + ["out"])
NSLOT = 3
assert len(USES) % NSLOT == 0
PER = len(USES) // NSLOT
ORDER = {name: n for n, name in enumerate(USES)}


def build(nc, x_in, consts_in, sel_in, w1_in, w2_in, out):
    ctx = ExitStack()
    with ctx:
        def sb(name, shape, dt=F32):
            return ctx.enter_context(nc.sbuf_tensor(name, shape, dt))

        def sem(name):
            return ctx.enter_context(nc.semaphore(name))

        xt = sb("xt", [P, 2, T])
        cst = sb("cst", [P, NCONST])
        pt = sb("pt", [P, 2, H, W])
        w1_stage = pt[:, :, :, :].rearrange("p c h n -> p (c h n)")[:, 0:2 * NF * P]
        sel = sb("sel", [P, H + 1 + NF, P], F32R)
        w1h = sb("w1h", [P, 2, NF, P], F32R)
        w1l = sb("w1l", [P, 2, NF, P], F32R)
        w2 = sb("w2", [P, NF, P])
        fpar = sb("fpar", [P, 7, NF])
        clt = sb("clt", [P, 3, 2 * NF])
        one = sb("one", [P, 1])
        eps = sb("eps", [P, 1])
        zbuf = sb("zbuf", [P, 2, 3, 2, T])
        zs, zmin = zbuf[:, 0, :, :, :], zbuf[:, 1, :, :, :]
        sel_stage = zbuf[:, :, :, :, :].rearrange("p a k s t -> p (a k s t)")[:, 0:(H + 1 + NF) * P]
        zrel = sb("zrel", [P, 2, T])
        zabs = sb("zabs", [P, 2, 2, T])
        t1 = sb("t1", [P, 2, T])
        t2 = sb("t2", [P, 2, T])
        diff = sb("diff", [P, 2, T])
        wlog = sb("wlog", [P, 2, T])
        rmax = sb("rmax", [P, 2, N])
        darg = sb("darg", [P, 2, 2, T])
        gh = sb("gh", [P, 2, T])
        dabs = sb("dabs", [P, 2, T])
        state = sb("state", [P, 2, T])
        h1 = sb("h1", [P, 2, W])
        h2 = sb("h2", [P, 2, W])
        xn = sb("xn", [P, 2, W])
        rstd = sb("rstd", [P, 2, W])
        qh = sb("qh", [P, 2, W], F32R)
        ql = sb("ql", [P, 2, W], F32R)
        kh = sb("kh", [P, 2, W], F32R)
        kl = sb("kl", [P, 2, W], F32R)
        qs = sb("qs", [96, 2, PAIRS, W], F32R)
        ks = sb("ks", [96, 2, PAIRS, 2, W], F32R)
        bq = sb("bq", [96, 2, 5 * P], F32R)
        bk = sb("bk", [96, 2, 5 * P], F32R)
        vpad = sb("vpad", [P, 2, 2, H, 32])
        vlast = sb("vlast", [P, 2, P])
        mx = sb("mx", [P, 2, 2, H])
        mxl = sb("mxl", [P, 2])
        nm = sb("nm", [P, 2, W], F32R)
        pl = sb("pl", [P, 2, W])
        rden = sb("rden", [P, 2, W])
        xh = sb("xh", [P, 2, W], F32R)
        xl = sb("xl", [P, 2, W], F32R)
        gl = sb("gl", [P, 4, CH, E])
        oh = sb("oh", [P, 2, CH, E])
        gm = sb("gm", [P, 8, CH])
        cw = sb("cw", [P, CH, NE])
        cwt1 = sb("cwt1", [P, CH, E])
        cwp = sb("cwp", [P, CH, P])
        cwt = sb("cwt", [P, 2, W], F32R)
        g0 = sb("g0", [P, 2, 2, W])
        u0 = sb("u0", [P, 2, 2, W])
        th = sb("th", [P, 2, 2, W])
        te = sb("te", [P, 2, 2, W])
        yo = sb("yo", [P, 2, W])
        osb = sb("osb", [P, CH, P])

        slot_mem = [ctx.enter_context(nc.psum_tensor(f"slot{i}", [P, 2, 512], F32)) for i in range(NSLOT)]
        acc = ctx.enter_context(nc.psum_tensor("acc", [P, 2, 512], F32))

        def const(name):
            a, b = CONSTS[name]
            return cst[:, a:b]

        ident = const("ident")
        par = const("par").rearrange("p (k c) -> p k c", c=NF)
        B1G, B1U, ALPHA, GSCALE, SHIFT, CLG, CLU = range(7)
        UB, HA, GHI, GLO, UHI, ULO, WSC = range(7)

        full = [sem(f"psum_full{i}") for i in range(NSLOT)]
        free = [sem(f"psum_free{i}") for i in range(NSLOT)]
        s_accfree = sem("acc_free")
        s_const, s_sel, s_w1, s_w2 = sem("const_loaded"), sem("sel_loaded"), sem("w1_loaded"), sem("w2_loaded")
        s_x, s_out = sem("x_loaded"), sem("out_stored")
        s_unit = sem("unit_done")
        s_init = sem("tiles_cleared")
        s_fit = sem("weights_ready")
        s_seta, s_setd = sem("act_setup"), sem("dve_setup")
        names = ("zs zmin zabs ezab lsp diff rmax darg edarg eh lh gh zrel dabs edabs ld fin efin t1 t2 wlog term "
                 "gsum state h1 sq lnv rstd xn qh ql kh kl vpad vlast stack bq bk mx mxl nm nml exp pl pv pvl lden rden att "
                 "h2 xh xl gate_l cwl gtop gexp cwp cwt g0 u0 gc uc th uw gg te ffn yo osb").split()
        S = {n: sem("r_" + n) for n in names}

        block = ctx.enter_context(nc.Block())

        def use(name):
            n = ORDER[name]
            return n % NSLOT, n // NSLOT

        def slot(name):
            return slot_mem[use(name)[0]]

        def take(eng, u, name):
            i, k = use(name)
            if k:
                eng.wait_ge(free[i], u * PER + k)

        def filled(eng, u, name):
            i, k = use(name)
            eng.wait_ge(full[i], u * PER + (k + 1))

        def released(eng, u, name):
            i, k = use(name)
            eng.wait_ge(free[i], u * PER + (k + 1))

        def fill(instr, name):
            instr.then_inc(full[use(name)[0]], 1)

        def release(instr, name):
            return instr.then_inc(free[use(name)[0]], 1)

        def units(eng):
            if LOOP:
                with eng.Fori(0, UNITS) as u:
                    yield u
            else:
                yield from range(UNITS)

        x_units = x_in.rearrange("p (u s t) -> u p s t", u=UNITS, s=2)
        out_units = out.rearrange("(s u) n c -> u s n c", s=2)

        @block.sync
        def _(sp):
            sp.dma_start(cst[:, :], consts_in).then_inc(s_const, 16)
            sp.dma_start(sel_stage, sel_in).then_inc(s_sel, 16)
            sp.dma_start(w1_stage, w1_in).then_inc(s_w1, 16)
            sp.dma_start(w2[:, :, :], w2_in.rearrange("p (c n) -> p c n", n=P)).then_inc(s_w2, 16)

            def unit(u):
                sp.wait_ge(s_unit, u + 1)
                sp.dma_start(xt[:, :, :], x_units[u]).then_inc(s_x, 16)
                sp.wait_ge(S["qh"], u + 1)
                released(sp, u, "q")
                for r, src in enumerate((qh, ql, qh)):
                    for t in range(PAIRS):
                        sp.dma_start(qs[32 * r:32 * r + 32, :, t, :].bitcast(F32), src[32 * t:32 * t + 32, :, :].bitcast(F32))\
                          .then_inc(S["stack"], 16)
                sp.wait_ge(S["kh"], u + 1)
                released(sp, u, "k")
                for r, src in enumerate((kh, kh, kl)):
                    for t in range(PAIRS):
                        for i in range(2):
                            sp.dma_start(ks[32 * r + 16 * i:32 * r + 16 * i + 16, :, t, i, :].bitcast(F32),
                                         src[32 * t + 16 * i:32 * t + 16 * i + 16, :, :].bitcast(F32))\
                              .then_inc(S["stack"], 16)
                sp.wait_ge(S["osb"], u + 1)
                released(sp, u, "out")
                for s in range(2):
                    dst = out_units[u]
                    sp.dma_start(dst[s, 0:256, :].rearrange("(c p) n -> p c n", p=P), osb[:, 2 * s:2 * s + 2, :])\
                      .then_inc(s_out, 16)
                    sp.dma_start(dst[s, 256:257, :], osb[ROWS[s]:ROWS[s] + 1, 4, :]).then_inc(s_out, 16)

            for u in range(UNITS):
                unit(u)
            sp.wait_ge(s_out, 64 * UNITS)
        STACK = 16 * 3 * PAIRS * 3

        @block.gpsimd
        def _(pool):
            for tile in (qs[:, :, :, :], ks[:, :, :, :, :], bq[:, :, :], bk[:, :, :], nm[:, :, :], cwt[:, :, :]):
                pool.memset(tile.bitcast(F32), 0.0).then_inc(s_init, 1)
            for tile in (vpad[:, :, :, :, :], cwp[:, :, :]):
                pool.memset(tile, 0.0).then_inc(s_init, 1)
            pool.memset(cw[:, :, E:NE], 1.0).then_inc(s_init, 1)
            pool.memset(one[:, :], 1.0).then_inc(s_init, 1)
            pool.memset(eps[:, :], EPS).then_inc(s_init, 1)
            pool.memset(h1[:, :, :], 0.5).then_inc(s_init, 1)
            pool.memset(rmax[:, :, 0:1], 0.0).then_inc(s_init, 1)
            pool.memset(h2[:, :, N:W], 0.5).then_inc(s_init, 1)
        INIT = 14

        @block.scalar
        def _(act):
            def tables(number):
                nc.scalar.add_instruction(mybir.InstLoadActFuncSet(
                    name=nc.get_next_instruction_name(), act_func_set_id=number, ins=[], outs=[]))

            a = nc.scalar.activation
            tables(SET_EXP_LN)
            act.wait_ge(s_init, INIT)
            act.wait_ge(s_const, 16)
            raw = par[:, CLG:CLU + 1, :].rearrange("p k c -> p (k c)")
            a(clt[:, 0, :], raw, ACT.Abs).then_inc(s_seta, 1)
            act.wait_ge(s_seta, 1)
            a(clt[:, 1, :], clt[:, 0, :], ACT.Exp, scale=-1.0).then_inc(s_seta, 1)
            act.wait_ge(s_seta, 2)
            a(clt[:, 2, :], clt[:, 1, :], ACT.Ln, bias=one[:, :]).then_inc(s_seta, 1)
            act.wait_ge(s_sel, 16)
            a(sel[:, :, :].rearrange("p c n -> p (c n)"), sel_stage, ACT.Copy).then_inc(s_seta, 1)
            act.wait_ge(s_w1, 16)
            a(w1h[:, :, :, :].rearrange("p k c n -> p (k c n)"), w1_stage, ACT.Copy).then_inc(s_seta, 1)

            def layernorm(u, which):
                filled(act, u, ("cent", which))
                a(rstd[:, :, :], slot(("cent", which))[:, :, 0:W], ACT.Square).then_inc(S["sq"], 1)
                filled(act, u, ("var", which))
                release(a(rstd[:, :, :], slot(("var", which))[:, :, 0:W], ACT.Ln, bias=eps[:, :])
                        , ("var", which))
                released(act, u, ("var", which))
                a(rstd[:, :, :], rstd[:, :, :], ACT.Exp, scale=-0.5).then_inc(S["rstd"], 1)

            def unit(u):
                tables(SET_EXP_LN)
                act.wait_ge(s_unit, u + 1)
                btok = const("btok")
                filled(act, u, "zfi")
                a(zs[:, 0, :, :].rearrange("p s t -> p (s t)"), slot("zfi")[:, 0, :], ACT.Identity,
                  bias=btok[:, 0:1]).then_inc(S["zs"], 1)
                release(a(zs[:, 1, :, :].rearrange("p s t -> p (s t)"), slot("zfi")[:, 1, :], ACT.Identity,
                          bias=btok[:, 1:2]), "zfi")
                filled(act, u, "zh")
                release(a(zs[:, 2, :, :].rearrange("p s t -> p (s t)"), slot("zh")[:, 0, :], ACT.Identity,
                          bias=btok[:, 2:3]), "zh")
                act.wait_ge(S["zs"], u + 1)
                released(act, u, "zfi")
                a(zabs[:, :, :, :], zs[:, 0:2, :, :], ACT.Abs).then_inc(S["zabs"], 1)
                act.wait_ge(S["zabs"], u + 1)
                a(zabs[:, :, :, :], zabs[:, :, :, :], ACT.Exp, scale=-1.0).then_inc(S["ezab"], 1)
                act.wait_ge(S["ezab"], u + 1)
                a(zabs[:, :, :, :], zabs[:, :, :, :], ACT.Ln, bias=one[:, :]).then_inc(S["lsp"], 1)
                act.wait_ge(S["zmin"], u + 1)
                a(gh[:, :, :], zmin[:, 2, :, :], ACT.Exp).then_inc(S["eh"], 1)
                act.wait_ge(S["eh"], u + 1)
                a(gh[:, :, :], gh[:, :, :], ACT.Ln, bias=one[:, :]).then_inc(S["lh"], 1)
                act.wait_ge(S["lh"], u + 1)
                a(gh[:, :, :], gh[:, :, :], ACT.Exp, scale=-1.0).then_inc(S["gh"], 1)
                act.wait_ge(S["diff"], u + 1)
                a(dabs[:, :, :], diff[:, :, :], ACT.Abs).then_inc(S["dabs"], 1)
                act.wait_ge(S["dabs"], u + 1)
                a(dabs[:, :, :], dabs[:, :, :], ACT.Exp, scale=-1.0).then_inc(S["edabs"], 1)
                act.wait_ge(S["edabs"], u + 1)
                a(dabs[:, :, :], dabs[:, :, :], ACT.Ln, bias=one[:, :]).then_inc(S["ld"], 1)
                act.wait_ge(S["darg"], 2 * u + 2)
                a(darg[:, :, :, :], darg[:, :, :, :], ACT.Exp).then_inc(S["edarg"], 1)
                act.wait_ge(S["fin"], u + 1)
                a(t2[:, :, :], t2[:, :, :], ACT.Exp).then_inc(S["efin"], 1)

                layernorm(u, 1)
                filled(act, u, "q")
                a(qh[:, :, :], slot("q")[:, :, 0:W], ACT.Copy).then_inc(S["qh"], 1)
                filled(act, u, "k")
                a(kh[:, :, :], slot("k")[:, :, 0:W], ACT.Copy).then_inc(S["kh"], 1)
                filled(act, u, "v")
                for s in range(2):
                    dst = vpad[:, s, :, :, :].rearrange("p c (j i) x -> p (c j) (i x)", i=2)
                    src = slot("v")[:, s, 0:256].rearrange("p (cj i x) -> p cj i x", i=2, x=DH)
                    for i in range(2):
                        last = a(dst[:, :, 48 * i:48 * i + DH], src[:, :, i, :], ACT.Copy)
                        last.then_inc(S["vpad"], 1)

                def negate_max(s):
                    filled(act, u, ("mlast", s))
                    a(nm[0:8, s, 0:256], slot(("mlast", s))[0:8, 1, 0:256], ACT.Copy, scale=-1.0)\
                        .then_inc(S["nm"], 1)

                def exps(s, c):
                    k = 2 * s + c
                    if k >= 2:
                        act.wait_ge(S["pv"], 4 * u + k - 1)
                    for t in range(PAIRS):
                        name = ("st", s, c, t)
                        filled(act, u, name)
                        ins = a(pt[:, c, 2 * t:2 * t + 2, :], slot(name)[:, :, 0:W], ACT.Exp, scale=SCORE_SCALE)
                        release(ins, name)

                def exp_last(s):
                    filled(act, u, ("plast", s))
                    release(a(pl[:, s, :], slot(("plast", s))[:, 0, 0:W], ACT.Exp, scale=SCORE_SCALE), ("plast", s))

                def reciprocal_den(s):
                    act.wait_ge(S["pv"], 4 * u + 2 * s + 2)
                    a(rden[:, s, :], acc[:, 1, 0:W], ACT.Ln).then_inc(S["lden"], 1)
                    act.wait_ge(S["lden"], 2 * u + s + 1)
                    a(rden[:, s, :], rden[:, s, :], ACT.Exp, scale=-1.0).then_inc(S["rden"], 1)

                negate_max(0)
                negate_max(1)
                exp_last(0)
                exps(0, 0)
                exps(0, 1)
                exp_last(1)
                exps(1, 0)
                reciprocal_den(0)
                exps(1, 1)
                reciprocal_den(1)

                layernorm(u, 2)
                released(act, u, ("cent", 2))
                a(xh[:, :, :], xn[:, :, :], ACT.Copy).then_inc(S["xh"], 1)
                tables(SET_EXP_TANH)
                act.wait_ge(S["gtop"], u + 1)
                a(gm[:, 5, :], gm[:, 4, :], ACT.Exp).then_inc(S["gexp"], 1)
                filled(act, u, "cwt")
                a(cwt[:, :, 0:256], slot("cwt")[:, 0, :].rearrange("p (s t) -> p s t", s=2), ACT.Copy)\
                    .then_inc(S["cwt"], 1)
                release(a(cwt[:, :, 256], slot("cwt")[:, 1, ROWS[0]:ROWS[1] + 1:ROWS[1] - ROWS[0]], ACT.Copy), "cwt")

                def evacuate(c):
                    p = c % 2
                    filled(act, u, ("g", c))
                    if c >= 2:
                        act.wait_ge(S["gg"], NF * u + c - 1)
                    release(a(g0[:, p, :, :], slot(("g", c))[:, :, 0:W], ACT.Identity, bias=par[:, B1G, c:c + 1]),
                            ("g", c))
                    filled(act, u, ("u", c))
                    if c >= 2:
                        act.wait_ge(S["te"], NF * u + c - 1)
                    release(a(u0[:, p, :, :], slot(("u", c))[:, :, 0:W], ACT.Identity, bias=fpar[:, UB, c:c + 1]),
                            ("u", c))

                def tanhs(c):
                    p = c % 2
                    act.wait_ge(S["gc"], NF * u + c + 1)
                    if c >= 2:
                        act.wait_ge(S["te"], NF * u + c - 1)
                    a(th[:, p, :, :], g0[:, p, :, :], ACT.Tanh, scale=fpar[:, HA, c:c + 1]).then_inc(S["th"], 1)

                for c in range(NF):
                    evacuate(c)
                    if c:
                        tanhs(c - 1)
                tanhs(NF - 1)

                filled(act, u, "out")
                for k in range(CH):
                    last = a(osb[:, k, :].rearrange("p (d h) -> p h d", h=H),
                             slot("out")[:, k // 4, (k % 4) * P:(k % 4 + 1) * P].rearrange("p (h d) -> p h d", h=H),
                             ACT.Copy)
                    if k == 3:
                        last.then_inc(S["osb"], 1)
                release(last, "out")

            act.wait_ge(s_fit, 1)
            if LOOP:
                with act.Fori(0, UNITS) as u:
                    unit(u)
            else:
                for u in range(UNITS):
                    unit(u)

        @block.vector
        def _(dve):
            v = nc.vector
            steps = [0]

            def then(ins):
                steps[0] += 1
                ins.then_inc(s_setd, 1)
                dve.wait_ge(s_setd, steps[0])

            dve.wait_ge(s_const, 16)
            dve.wait_ge(s_seta, 3)
            raw = par[:, CLG:CLU + 1, :].rearrange("p k c -> p (k c)")
            then(v.scalar_tensor_tensor(clt[:, 0, :], raw, 0.0, clt[:, 2, :], ALU.max, ALU.add))
            cg, cu = clt[:, 0, 0:NF], clt[:, 0, NF:2 * NF]
            then(v.tensor_copy(fpar[:, GHI, :], cg))
            then(v.tensor_scalar(fpar[:, GLO, :], cg, -1.0, None, ALU.mult))
            then(v.tensor_tensor(fpar[:, UHI, :], par[:, SHIFT, :], cu, ALU.add))
            then(v.tensor_tensor(fpar[:, ULO, :], par[:, SHIFT, :], cu, ALU.subtract))
            then(v.tensor_tensor(fpar[:, UB, :], par[:, B1U, :], par[:, SHIFT, :], ALU.add))
            then(v.tensor_scalar(fpar[:, HA, :], par[:, ALPHA, :], 0.5, None, ALU.mult))
            then(v.tensor_scalar(fpar[:, WSC, :], par[:, GSCALE, :], 0.5, None, ALU.mult))
            dve.wait_ge(s_w2, 16)
            then(v.tensor_tensor(w2[:, :, :], w2[:, :, :], fpar[:, WSC, :].unsqueeze(2).to_broadcast([P, NF, P]),
                                 ALU.mult))
            dve.wait_ge(s_seta, 5)
            dve.wait_ge(s_w1, 16)
            then(v.tensor_tensor(w1l[:, :, :, :].rearrange("p k c n -> p (k c n)"), w1_stage,
                                 w1h[:, :, :, :].rearrange("p k c n -> p (k c n)").bitcast(F32), ALU.subtract))
            dve.wait_ge(s_init, INIT)
            v.memset(clt[:, 1, 0:1], 0.0).then_inc(s_fit, 1)

            def first(eng_sem, value):
                dve.wait_ge(S[eng_sem], value)

            def layernorm(u, which):
                first("rstd", 2 * u + which)
                filled(dve, u, ("cent", which))
                ins = v.tensor_tensor(xn[:, :, :], slot(("cent", which))[:, :, 0:W], rstd[:, :, :], ALU.mult)
                release(ins, ("cent", which))

            def unit(u):
                dve.wait_ge(s_unit, u + 1)
                released(dve, u, "zh")
                released(dve, u, "zfi")
                dve.wait_ge(S["zs"], u + 1)
                v.tensor_scalar(zmin, zs, 0.0, None, ALU.min).then_inc(S["zmin"], 1)
                v.tensor_scalar(zrel[:, :, :], zs[:, 2, :, :], 0.0, None, ALU.max).then_inc(S["zrel"], 1)
                first("zmin", u + 1)
                v.tensor_tensor(t2[:, :, :], zmin[:, 1, :, :], zmin[:, 0, :, :], ALU.subtract).then_inc(S["t2"], 1)
                first("lsp", u + 1)
                v.tensor_tensor(t1[:, :, :], zabs[:, 0, :, :], zabs[:, 1, :, :], ALU.subtract).then_inc(S["t1"], 1)
                first("t1", 2 * u + 1)
                first("t2", u + 1)
                v.tensor_tensor(diff[:, :, :], t1[:, :, :], t2[:, :, :], ALU.add).then_inc(S["diff"], 1)
                first("diff", u + 1)
                v.tensor_tensor(wlog[:, :, :], diff[:, :, :], zmin[:, 2, :, :], ALU.add).then_inc(S["wlog"], 1)
                first("wlog", u + 1)
                for s in range(2):
                    v.tensor_tensor_scan(rmax[:, s, 1:N], wlog[:, s, :], wlog[:, s, :], 0.0, ALU.max, ALU.max)\
                        .then_inc(S["rmax"], 1)
                first("rmax", 2 * u + 2)
                v.tensor_tensor(darg[:, 0, :, :], rmax[:, :, 0:T], rmax[:, :, 1:N], ALU.subtract)\
                    .then_inc(S["darg"], 1)
                v.tensor_tensor(darg[:, 1, :, :], wlog[:, :, :], rmax[:, :, 1:N], ALU.subtract)\
                    .then_inc(S["darg"], 1)
                first("gh", u + 1)
                first("zrel", u + 1)
                v.tensor_tensor(gh[:, :, :], gh[:, :, :], zrel[:, :, :], ALU.add).then_inc(S["gsum"], 1)
                first("ld", u + 1)
                v.scalar_tensor_tensor(t1[:, :, :], diff[:, :, :], 0.0, dabs[:, :, :], ALU.max, ALU.add)\
                    .then_inc(S["t1"], 1)
                first("edarg", u + 1)
                first("gsum", u + 1)
                v.tensor_tensor(gh[:, :, :], darg[:, 1, :, :], gh[:, :, :], ALU.mult).then_inc(S["term"], 1)
                first("t1", 2 * u + 2)
                first("term", u + 1)
                v.tensor_tensor(t2[:, :, :], rmax[:, :, 1:N], t1[:, :, :], ALU.subtract).then_inc(S["fin"], 1)
                for s in range(2):
                    v.tensor_tensor_scan(state[:, s, :], darg[:, 0, s, :], gh[:, s, :], 0.5, ALU.mult, ALU.add)\
                        .then_inc(S["state"], 1)
                first("state", 2 * u + 2)
                first("efin", u + 1)
                v.tensor_tensor(h1[:, :, 1:N], t2[:, :, :], state[:, :, :], ALU.mult).then_inc(S["h1"], 1)

                layernorm(u, 1)
                for name, hi, lo in (("q", qh, ql), ("k", kh, kl)):
                    filled(dve, u, name)
                    first(name + "h", u + 1)
                    release(v.tensor_tensor(lo[:, :, :], slot(name)[:, :, 0:W], hi[:, :, :].bitcast(F32), ALU.subtract),
                            name)
                filled(dve, u, "v")
                first("vpad", 4 * u + 4)
                release(v.tensor_tensor(vlast[:, :, :], slot("v")[:, :, 256:384],
                                        const("mask8").unsqueeze(1).to_broadcast([P, 2, P]), ALU.mult),
                        "v")

                first("stack", STACK * (u + 1))
                for s in range(2):
                    dq = bq[:, s, 0:4 * 130].rearrange("p (t x) -> p t x", x=130)[:, :, 0:2]
                    v.tensor_tensor(dq, qs[:, s, :, 256:257].bitcast(F32).to_broadcast([96, PAIRS, 2]),
                                    const("maskp")[0:96, :].unsqueeze(1).to_broadcast([96, PAIRS, 2]), ALU.mult)\
                        .then_inc(S["bq"], 1)
                    dk = bk[:, s, 0:4 * 130].rearrange("p (t x) -> p t x", x=130)[:, :, 0:2]
                    v.tensor_copy(dk, ks[:, s, :, :, 256].bitcast(F32)).then_inc(S["bk"], 1)

                for name in MAXES:
                    _, s, c, t = name
                    filled(dve, u, name)
                    release(v.tensor_reduce(mx[:, s, c, 2 * t:2 * t + 2], slot(name)[:, :, 0:N], AX_X, ALU.max), name)
                for s in range(2):
                    name = ("mlast", s)
                    filled(dve, u, name)
                    first("nm", 2 * u + s + 1)
                    release(v.tensor_reduce(mxl[:, s:s + 1], slot(name)[:, 0, 0:N], AX_X, ALU.max), name)
                    released(dve, u, name)
                    v.tensor_scalar(nm[:, s, 256:257], mxl[:, s:s + 1], -1.0, None, ALU.mult).then_inc(S["nml"], 1)
                for s in range(2):
                    first("rden", 2 * u + s + 1)
                    v.tensor_tensor(rden[:, s, :], acc[:, 0, 0:W], rden[:, s, :], ALU.mult).then_inc(s_accfree, 1)
                    dve.wait_ge(s_accfree, 3 * u + s + 1)
                    v.tensor_tensor(h2[:, s, 0:N], rden[:, s, 0:N], h1[:, s, 0:N], ALU.add).then_inc(S["h2"], 1)

                layernorm(u, 2)
                released(dve, u, ("cent", 2))
                first("xh", u + 1)
                v.tensor_tensor(xl[:, :, :], xn[:, :, :], xh[:, :, :].bitcast(F32), ALU.subtract)\
                    .then_inc(S["xl"], 1)

                count = [0]

                def small(ins):
                    count[0] += 1
                    ins.then_inc(S["cwl"], 1)
                    dve.wait_ge(S["cwl"], u * SMALL + count[0])

                def wide(ap):
                    return ap.unsqueeze(2).to_broadcast([P, CH, E])

                rank = const("rank").unsqueeze(1).to_broadcast([P, CH, E])
                filled(dve, u, "gate")
                release(v.tensor_tensor(gl[:, 0, :, :], slot("gate")[:, 0, 0:CH * E].rearrange("p (k e) -> p k e", e=E),
                                        const("gate_b").unsqueeze(1).to_broadcast([P, CH, E]), ALU.add), "gate")
                released(dve, u, "gate")
                for r in range(2):
                    small(v.tensor_reduce(gm[:, r, :], gl[:, r, :, :], AX_X, ALU.max))
                    small(v.tensor_tensor(gl[:, 2, :, :], gl[:, r, :, :], wide(gm[:, r, :]), ALU.is_equal))
                    small(v.tensor_tensor(gl[:, 3, :, :], gl[:, 2, :, :], rank, ALU.mult))
                    small(v.tensor_reduce(gm[:, 2 + r, :], gl[:, 3, :, :], AX_X, ALU.max))
                    small(v.tensor_tensor(oh[:, r, :, :], rank, wide(gm[:, 2 + r, :]), ALU.is_equal))
                    if r == 0:
                        small(v.scalar_tensor_tensor(gl[:, 1, :, :], oh[:, 0, :, :], -1e30, gl[:, 0, :, :],
                                                     ALU.mult, ALU.add))
                v.tensor_tensor(gm[:, 4, :], gm[:, 1, :], gm[:, 0, :], ALU.subtract).then_inc(S["gtop"], 1)
                first("gexp", u + 1)
                small(v.tensor_scalar(gm[:, 6, :], gm[:, 5, :], 1.0, None, ALU.add))
                small(v.reciprocal(gm[:, 7, :], gm[:, 6, :]))
                small(v.tensor_tensor(gm[:, 6, :], gm[:, 5, :], gm[:, 7, :], ALU.mult))
                small(v.tensor_tensor(cw[:, :, 0:E], oh[:, 0, :, :], wide(gm[:, 7, :]), ALU.mult))
                small(v.tensor_tensor(cwt1[:, :, :], oh[:, 1, :, :], wide(gm[:, 6, :]), ALU.mult))
                small(v.tensor_tensor(cw[:, :, 0:E], cw[:, :, 0:E], cwt1[:, :, :], ALU.add))
                small(v.tensor_copy(cwp[:, :, 0:NE].bitcast(F32R), cw[:, :, :]))
                v.tensor_tensor(cwp[:, :, 32:32 + NE], cw[:, :, :], cwp[:, :, 0:NE], ALU.subtract)\
                    .then_inc(S["cwp"], 1)

                def clips(c):
                    p = c % 2
                    released(dve, u, ("g", c))
                    v.tensor_scalar(g0[:, p, :, :], g0[:, p, :, :], fpar[:, GHI, c:c + 1], fpar[:, GLO, c:c + 1],
                                    ALU.min, ALU.max).then_inc(S["gc"], 1)
                    released(dve, u, ("u", c))
                    v.tensor_scalar(u0[:, p, :, :], u0[:, p, :, :], fpar[:, UHI, c:c + 1], fpar[:, ULO, c:c + 1],
                                    ALU.min, ALU.max).then_inc(S["uc"], 1)

                def products(c):
                    p = c % 2
                    filled(dve, u, ("cw", c))
                    first("uc", NF * u + c + 1)
                    release(v.tensor_tensor(u0[:, p, :, :], slot(("cw", c))[:, :, 0:W], u0[:, p, :, :], ALU.mult),
                            ("cw", c))
                    first("th", NF * u + c + 1)
                    v.scalar_tensor_tensor(th[:, p, :, :], th[:, p, :, :], 1.0, g0[:, p, :, :], ALU.add, ALU.mult)\
                        .then_inc(S["gg"], 1)
                    first("gg", NF * u + c + 1)
                    released(dve, u, ("cw", c))
                    if c >= 2:
                        first("ffn", NF * u + c - 1)
                    v.tensor_tensor(te[:, p, :, :], th[:, p, :, :], u0[:, p, :, :], ALU.mult).then_inc(S["te"], 1)

                for c in range(NF):
                    clips(c)
                    if c:
                        products(c - 1)
                products(NF - 1)
                first("ffn", NF * u + NF)
                v.tensor_tensor(yo[:, :, :], acc[:, :, 0:W], h2[:, :, :], ALU.add).then_inc(s_accfree, 1)
            SMALL = 18

            v.memset(clt[:, 1, 1:2], 0.0).then_inc(s_unit, 1)
            if LOOP:
                with dve.Fori(0, UNITS) as u:
                    unit(u)
                    dve.wait_ge(s_out, 64 * u + 64)
                    v.memset(clt[:, 1, 1:2], 0.0).then_inc(s_unit, 1)
            else:
                for u in range(UNITS):
                    unit(u)
                    dve.wait_ge(s_out, 64 * u + 64)
                    v.memset(clt[:, 1, 1:2], 0.0).then_inc(s_unit, 1)

        @block.tensor
        def _(pe):
            def mm(out_, lhsT, rhs, start=True, stop=True, **k):
                return nc.tensor.matmul(out_, lhsT, rhs, start=start, stop=stop, **k)

            def layernorm(u, which, src):
                name = ("cent", which)
                take(pe, u, name)
                for s in range(2):
                    last = mm(slot(name)[:, s, 0:W], const("cmat"), src[:, s, :])
                fill(last, name)
                name = ("var", which)
                take(pe, u, name)
                pe.wait_ge(S["sq"], 2 * u + which)
                for s in range(2):
                    last = mm(slot(name)[:, s, 0:W], const("omat"), rstd[:, s, :])
                fill(last, name)

            def unit(u):
                pe.wait_ge(s_unit, u + 1)
                pe.wait_ge(s_x, 16 * (u + 1))
                wtok = const("wtok").rearrange("p (k n) -> p k n", n=P)
                xall = xt[:, :, :].rearrange("p s t -> p (s t)")
                for k in range(2):
                    last = mm(slot("zfi")[:, k, :], wtok[:, k, :], xall)
                fill(last, "zfi")
                fill(mm(slot("zh")[:, 0, :], wtok[:, 2, :], xall), "zh")
                pe.wait_ge(S["h1"], u + 1)
                layernorm(u, 1, h1)
                released(pe, u, ("cent", 1))
                for name in ("q", "k"):
                    take(pe, u, name)
                    for s in range(2):
                        last = mm(slot(name)[:, s, 0:W], const("w" + name), xn[:, s, :])
                    fill(last, name)
                take(pe, u, "v")
                for s in range(2):
                    for c in range(2):
                        mm(slot("v")[:, s, c * P:(c + 1) * P], xn[:, s, c * P:(c + 1) * P], const("wv"))
                    last = mm(slot("v")[:, s, 256:384], xn[:, s, 256:257].to_broadcast([P, P]), const("wv"))
                fill(last, "v")

                pe.wait_ge(S["stack"], STACK * (u + 1))
                for name in MAXES:
                    _, s, c, t = name
                    take(pe, u, name)
                    for i in range(2):
                        last = mm(slot(name)[:, i, 0:W], qs[:, s, t, c * P:(c + 1) * P], ks[:, 1 - s, t, i, :])
                    fill(last, name)
                for s in range(2):
                    name = ("mlast", s)
                    take(pe, u, name)
                    pe.wait_ge(S["bq"], 2 * u + 2)
                    for t in range(PAIRS):
                        for i in range(2):
                            k = 2 * t + i
                            mm(slot(name)[:, 0, 0:W], bq[:, s, t * P:(t + 1) * P], ks[:, 1 - s, t, i, :],
                               start=(k == 0), stop=(k == H - 1))
                    for m in MAXES[8 * s + 5:8 * s + 8]:
                        released(pe, u, m)
                    for c in range(2):
                        last = mm(slot(name)[0:8, 1, c * P:(c + 1) * P], mx[:, s, c, :], ident)
                    fill(last, name)

                def scores_last(s):
                    name = ("plast", s)
                    take(pe, u, name)
                    pe.wait_ge(S["nm"], 2 * u + s + 1)
                    pe.wait_ge(S["nml"], 2 * u + s + 1)
                    pe.wait_ge(S["bk"], 2 * u + 2)
                    for t in range(PAIRS):
                        mm(slot(name)[:, 0, 0:W], bk[:, 1 - s, t * P:(t + 1) * P], qs[:, s, t, :],
                           start=(t == 0), stop=False)
                    fill(mm(slot(name)[:, 0, 0:W], sel[:, H, :], nm[:, s, :], start=False), name)

                def scores_t(s, c):
                    for t in range(PAIRS):
                        name = ("st", s, c, t)
                        take(pe, u, name)
                        for i in range(2):
                            mm(slot(name)[:, i, 0:W], ks[:, 1 - s, t, i, c * P:(c + 1) * P], qs[:, s, t, :], stop=False)
                            last = mm(slot(name)[:, i, 0:W], sel[:, 2 * t + i, :], nm[:, s, :], start=False)
                        fill(last, name)

                def values_last(s):
                    if s:
                        pe.wait_ge(s_accfree, 3 * u + s)
                    released(pe, u, ("plast", s))
                    released(pe, u, "v")
                    mm(acc[:, 0, 0:W], vlast[:, 1 - s, :], pl[:, s, :], stop=False)
                    mm(acc[:, 1, 0:W], const("mask8"), pl[:, s, :], stop=False)

                def values(s, c):
                    for t in range(PAIRS):
                        released(pe, u, ("st", s, c, t))
                    ones32 = const("ones32")
                    for i in range(2):
                        end = c == 1 and i == 1
                        for bank in range(2):
                            for t in range(PAIRS):
                                lhsT = ones32[:, 32 * i:32 * i + 32] if bank else vpad[:, 1 - s, c, 2 * t + i, :]
                                last = mm(acc[32 * t:32 * t + 32, bank, 0:W], lhsT, pt[:, c, 2 * t + i, :],
                                          start=False, stop=end)
                    last.then_inc(S["pv"], 1)

                scores_last(0)
                scores_t(0, 0)
                pe.wait_ge(S["vpad"], 4 * u + 4)
                scores_t(0, 1)
                values_last(0)
                values(0, 0)
                scores_last(1)
                scores_t(1, 0)
                values(0, 1)
                scores_t(1, 1)
                values_last(1)
                values(1, 0)
                values(1, 1)

                pe.wait_ge(S["h2"], 2 * u + 2)
                layernorm(u, 2, h2)
                released(pe, u, ("cent", 2))
                take(pe, u, "gate")
                for k in range(CH):
                    s, c = divmod(k, 2)
                    lhsT = (xn[:, s, c * P:(c + 1) * P] if k < 4
                            else xn[:, :, :].rearrange("p s t -> p (s t)")[:, LAST])
                    last = mm(slot("gate")[:, 0, k * E:(k + 1) * E], lhsT, const("gate_w"))
                fill(last, "gate")

                def up(c):
                    if c == 0:
                        pe.wait_ge(S["xl"], u + 1)
                    for k, name in enumerate((("g", c), ("u", c))):
                        take(pe, u, name)
                        for s in range(2):
                            o = slot(name)[:, s, 0:W]
                            mm(o, w1h[:, k, c, :], xh[:, s, :], stop=False)
                            mm(o, w1h[:, k, c, :], xl[:, s, :], start=False, stop=False)
                            last = mm(o, w1l[:, k, c, :], xh[:, s, :], start=False)
                        fill(last, name)

                def weights_of(c):
                    name = ("cw", c)
                    take(pe, u, name)
                    for s in range(2):
                        last = mm(slot(name)[:, s, 0:W], sel[:, H + 1 + c, :], cwt[:, s, :])
                    fill(last, name)

                def down(c):
                    pe.wait_ge(S["te"], NF * u + c + 1)
                    for s in range(2):
                        last = mm(acc[:, s, 0:W], w2[:, c, :], te[:, c % 2, s, :], start=False, stop=(c == NF - 1))
                    last.then_inc(S["ffn"], 1)

                take(pe, u, "cwt")
                pe.wait_ge(S["cwp"], u + 1)
                for k in range(CH):
                    last = nc.tensor.transpose(slot("cwt")[:, k // 4, (k % 4) * P:(k % 4 + 1) * P], cwp[:, k, :], ident)
                fill(last, "cwt")
                up(0)
                released(pe, u, "cwt")
                pe.wait_ge(S["cwt"], u + 1)
                pe.wait_ge(s_accfree, 3 * u + 2)
                for s in range(2):
                    mm(acc[:, s, 0:W], const("b2"), cwt[:, s, :].bitcast(F32), stop=False)
                weights_of(0)
                for c in range(1, NF):
                    up(c)
                    weights_of(c)
                    down(c - 1)
                down(NF - 1)
                take(pe, u, "out")
                pe.wait_ge(s_accfree, 3 * u + 3)
                for k in range(CH):
                    s, c = divmod(k, 2)
                    src = yo[:, s, c * P:(c + 1) * P] if k < 4 else yo[:, :, :].rearrange("p s t -> p (s t)")[:, LAST]
                    last = nc.tensor.matmul(slot("out")[:, k // 4, (k % 4) * P:(k % 4 + 1) * P], src, ident,
                                            is_transpose=True, start=True, stop=True)
                fill(last, "out")

            pe.wait_ge(s_fit, 1)
            pe.wait_ge(s_seta, 4)
            if LOOP:
                with pe.Fori(0, UNITS) as u:
                    unit(u)
            else:
                for u in range(UNITS):
                    unit(u)


def layout(inputs):
    f = lambda n: np.asarray(inputs[n])
    j = np.arange(P)
    perm = (j % DH) * H + j // DH
    x = f("x")[[0, 4, 1, 5, 2, 6, 3, 7]].transpose(2, 0, 1).reshape(P, B * T)

    feats = NF * P
    expert_of = np.minimum(np.arange(feats) // I, NE)

    def per_feature(shared, expert):
        v = np.concatenate([np.asarray(expert).reshape(E), np.asarray(shared).reshape(1), np.zeros(1, np.float32)])
        return v[expert_of].reshape(NF, P).T

    def features(a):
        v = np.concatenate([a.reshape(-1), np.zeros(feats - NE * I, np.float32)])
        return v.reshape(NF, P).T

    b1 = np.concatenate([f("L0_ffn_expert_b1"), f("L0_ffn_shared_b1")[None]])
    ea, sa = f("L0_ffn_expert_act"), f("L0_ffn_shared_act")
    params = [features(b1[:, 0::2]), features(b1[:, 1::2])] + [per_feature(sa[k], ea[:, k]) for k in range(5)]
    w1 = np.concatenate([f("L0_ffn_expert_w1"), f("L0_ffn_shared_w1")[None]])[:, perm, :]
    w1 = w1.transpose(1, 0, 2)
    pad = np.zeros((P, feats - NE * I), np.float32)
    w1 = np.concatenate([w1[:, :, 0::2].reshape(P, -1), pad, w1[:, :, 1::2].reshape(P, -1), pad], axis=1)
    w2 = np.concatenate([f("L0_ffn_expert_w2"), f("L0_ffn_shared_w2")[None]])[:, :, perm].reshape(NE * I, D)
    w2 = np.concatenate([w2, pad.T]).reshape(NF, P, D).transpose(1, 0, 2).reshape(P, NF * D)
    b2 = np.concatenate([f("L0_ffn_expert_b2"), f("L0_ffn_shared_b2")[None]])[:, perm]
    b2s = np.zeros((P, P), np.float32)
    b2s[0:NE] = b2
    b2s[32:32 + NE] = b2

    eye = np.eye(P, dtype=np.float32)
    zero16 = np.zeros((P, DH), np.float32)
    one16 = np.ones((P, DH), np.float32)
    mask8 = np.zeros((P, P), np.float32)
    mask8[j // DH, j] = 1.0
    maskp = np.stack([(j // DH) % 2 == 0, (j // DH) % 2 == 1], axis=1).astype(np.float32)
    parts = {
        "wtok": np.concatenate([f(n)[:, perm] for n in ("L0_tok_Wf", "L0_tok_Wi", "L0_tok_Wh")], axis=1),
        "btok": np.stack([f(n)[perm] for n in ("L0_tok_bf", "L0_tok_bi", "L0_tok_bh")], axis=1),
        "cmat": eye - np.float32(1.0 / P), "omat": np.full((P, P), 1.0 / P, np.float32),
        "wq": f("L0_attn_q_w")[:, perm].T, "wk": f("L0_attn_kv_w")[:D, perm].T, "wv": f("L0_attn_kv_w")[D:, perm].T,
        "ident": eye, "ones32": np.concatenate([one16, zero16, zero16, one16], axis=1), "mask8": mask8,
        "maskp": maskp, "gate_w": f("L0_ffn_gate_w")[perm], "gate_b": np.repeat(f("L0_ffn_gate_b")[None], P, axis=0),
        "rank": np.repeat(np.arange(E, 0, -1, dtype=np.float32)[None], P, axis=0), "b2": b2s,
        "par": np.concatenate(params, axis=1),
    }
    consts = np.concatenate([parts[n] for n in CONSTS], axis=1)
    sel = np.zeros((P, H + 1 + NF, P), np.float32)
    for h in range(H):
        sel[h, h, :] = 1.0
        sel[h, H, h] = 1.0
    for n in range(NE * I):
        sel[n // I, H + 1 + n // P, n % P] = 1.0
        sel[32 + n // I, H + 1 + n // P, n % P] = 1.0
    arrays = {"x": x, "consts": consts, "sel": sel.reshape(P, -1), "w1": w1, "w2": w2}
    return {k: np.ascontiguousarray(a) for k, a in arrays.items()}


def kernel(**inputs):
    import concourse.bacc as bacc
    from concourse.bass_utils import run_bass_kernel_spmd

    nc = bacc.Bacc("TRN2", target_bir_lowering=False, num_devices=1)
    arrays = {f"in_{k}": a for k, a in layout(inputs).items()}
    args = [nc.dram_tensor(k, a.shape, mybir.dt.from_np(a.dtype), kind="ExternalInput").ap() for k, a in arrays.items()]
    out = nc.dram_tensor("out", (B, N, D), F32, kind="ExternalOutput").ap()
    build(nc, *args, out)
    r = run_bass_kernel_spmd(nc, [arrays], core_ids=[0])
    return r.results[0]["out"]
```

```python
from contextlib import ExitStack

import numpy as np
import concourse.bass as bass
from concourse import mybir

F32 = mybir.dt.float32
F32R = mybir.dt.float32r
ALU = mybir.AluOpType
ACT = mybir.ActivationFunctionType
AX_X = mybir.AxisListType.X

P = 128
B, T, D = 8, 256, 128
N = T + 1
W = N + 1
UNITS = B // 2
H, DH = 8, 16
PAIRS = H // 2
E, I = 16, 96
NE = E + 1
NF = -(-NE * I // P)
CH = 5
SCORE_SCALE = float(D) ** -0.5
EPS = 1e-5
SET_EXP_LN = 6
SET_EXP_TANH = 0
STEP = 3
LAST = slice(2 * W - 2 - STEP * (P - 1), 2 * W - 1, STEP)
ROWS = ((N - 1 - LAST.start) // STEP, P - 1)

CONSTS = {}
_at = 0
for _name, _n in (("wtok", 3 * P), ("btok", 3), ("cmat", P), ("omat", P), ("wq", P), ("wk", P), ("wv", P),
                  ("ident", P), ("ones32", 64), ("mask8", P), ("maskp", 2), ("hot", H), ("gate_w", E),
                  ("gate_b", E), ("rank", E), ("b2", P), ("par", 7 * NF)):
    CONSTS[_name] = (_at, _at + _n)
    _at += _n
NCONST = _at
NFIRST = CONSTS["wq"][0]
KR = 96
NSLOT = 4


NB = 3
NTE = 8
BURSTS = ((0, 4), (4, 8), (8, NF))
ROUTE = 5


FEED = {'g': 0.0, 'clip_up_1': 0.11, 'u': 0.4, 'gated_1': 0.5, 'cw_1': 0.7, 'clip_gate': 0.65}
DOWN = (5.95, 10.26, 13.93)
ADD = (6.22, 10.25, 14.85)
ATTEND = {'begin': 0.0, 'max': 0.21, 'st': 0.18, 'mlast': 0.2, 'mtop': 0.05, 'plast': 0.2, 'pv': 0.2, 'norm': 0.2}
TOKEN = (-0.27, 1.97, 2.09, 2.69, 3.78, 5.2, 6.2, 7.14, 7.4, 8.2)
NORM_A = {'center': 9.1, 'variance': 10.05, 'scale': 11.1, 'gate': 11.2}
NORM_T = {'center': 9.11, 'variance': 10.11, 'scale': 11.11, 'project': 11.43}
ROUTING = (12.16, 13.66, 14.06, 14.17, 14.27)
LATE = {'split': 15.0, 'cwt': 15.0, 'keep': 15.34}
OUT = 16.51
TOKEN_ALONE = (-1.0, -0.9, -0.8, -0.7, 0.97, 1.97, 2.97, 4.81, 4.97, 9.05)


def attention_pieces():
    st = lambda s: [("st", s, c, t) for c in range(2) for t in range(PAIRS)]
    mx = lambda s: [("max", s, c, t) for c in range(2) for t in range(PAIRS)]
    mixed = [p for pair in zip(mx(1), st(0)) for p in pair]
    return (mx(0) + [("mlast", 0)] + mx(1)[:1] + [("mtop", 0)] + mx(1)[1:3] + [("plast", 0)] + mx(1)[3:4] + st(0)[:4]
            + mixed[8:] + [("mlast", 1), ("pv", 0), ("mtop", 1), ("plast", 1), ("norm", 0)] + st(1)
            + [("pv", 1), ("norm", 1)])


def plan(f, a, t):
    at = []
    if f:
        for c in range(NF + 1):
            for name, when in FEED.items():
                before = name.endswith("_1")
                if 0 <= c - before < NF:
                    at.append((c + when, "F", name.removesuffix("_1"), c - before))
        at += [(when, "F", "down", b) for b, when in enumerate(DOWN)] + [(when, "F", "add", b) for b, when in enumerate(ADD)]
        at.append((OUT, "F", "out"))
    if a:
        when = ATTEND["begin"]
        for name, *numbers in attention_pieces():
            at.append((when, "A", name, *numbers))
            when += ATTEND[name]
        at += [(when, "A", name, *((2,) if name != "gate" else ())) for name, when in NORM_A.items()]
        at += [(when, "A", "route", k) for k, when in enumerate(ROUTING)] + [(when, "A", name) for name, when in LATE.items()]
    if t:
        at += [(when, "T", "token", k) for k, when in enumerate(TOKEN if f else TOKEN_ALONE)]
        at += [(when, "T", name, *((1,) if name != "project" else ())) for name, when in NORM_T.items()]
    return [piece for _, *piece in sorted(at, key=lambda x: x[0])]


SLOTS_OF = {"g": ("g",), "u": ("u",), "cw": ("cw",), "max": ("max",), "mlast": ("mlast",), "plast": ("plast",),
            "st": ("st",), "pv": ("pv",), "center": ("cent",), "variance": ("var",), "scale": ("xc",), "project": ("q", "k", "v0", "v1"),
            "gate": ("gate",), "cwt": ("cwt",), "down": ("down",),
            "out": ("out",)}


def slot_uses(pieces):
    uses = []
    for _, piece, *numbers in pieces:
        names = ("zf", "zi", "zh") if (piece, numbers) == ("token", [0]) else SLOTS_OF.get(piece, ())
        uses += [(n, *numbers) if piece != "token" else (n,) for n in names]
    return uses


STEPS = {-2: (0, 0, 1), -1: (0, 1, 1), 0: (1, 1, 1), 2: (1, 1, 0), 3: (1, 0, 0)}
LOOPED = UNITS - 2
PLANS = {i: plan(*stages) for i, stages in STEPS.items()}
USES = {i: {name: n for n, name in enumerate(slot_uses(p))} for i, p in PLANS.items()}
assert len(USES[0]) % NSLOT == 0
BASE = {}
_at = 0
for _i in STEPS:
    BASE[_i] = _at
    _at += len(USES[_i]) * (LOOPED if _i == 0 else 1)


class Step:

    def __init__(self, kind, i):
        self.kind, self.i = kind, i
        self.plan = PLANS[kind]

    def unit(self, stage):
        return self.i + {"F": 0, "A": 1, "T": 2}[stage]

    def use(self, name):
        n = BASE[self.kind] + USES[self.kind][name]
        before = n // NSLOT
        if self.kind == 0:
            before = self.i * (len(USES[0]) // NSLOT) + before
        return n % NSLOT, before


def build(nc, x_in, consts_in, sel_in, w1_in, w2_in, spill, out):
    ctx = ExitStack()
    with ctx:
        def sb(name, shape, dt=F32):
            return ctx.enter_context(nc.sbuf_tensor(name, shape, dt))

        def sem(name):
            return ctx.enter_context(nc.semaphore(name))

        cst = sb("cst", [P, NCONST])
        sel = sb("sel", [P, NF, P], F32R)
        w1h = sb("w1h", [P, 2, NF, P], F32R)
        w1l = sb("w1l", [P, 2, NF, P], F32R)
        w2 = sb("w2", [P, NF, P])
        fpar = sb("fpar", [P, 7, NF])
        clt = sb("clt", [P, 3, 2 * NF])
        one = sb("one", [P, 1])
        eps = sb("eps", [P, 1])
        credit = sb("credit", [P, 1])
        xt = sb("xt", [P, 2, T])
        zs = sb("zs", [P, 3, 2, T])
        earg = zs
        fexp = sb("fexp", [P, 2, T])
        zmin = sb("zmin", [P, 3, 2, T])
        zpos = sb("zpos", [P, 2, T])
        zabs = sb("zabs", [P, 2, 2, T])
        xn1 = sb("xn1", [P, 2, W])
        stat1 = sb("stat1", [P, 2, W])
        dlog, wlog = xn1[:, :, 0:T], stat1[:, :, 0:T]
        drel = sb("drel", [P, 2, T])
        rmax = sb("rmax", [P, 2, N])
        half = sb("half", [P, 2, T])
        gate = sb("gate", [P, 2, T])
        state = sb("state", [P, 2, T])
        h1 = sb("h1", [P, 2, W])
        qhl = sb("qhl", [P, 2, 2, W], F32R)
        khl = sb("khl", [P, 2, 2, W], F32R)
        qh, ql, kh, kl = qhl[:, 0], qhl[:, 1], khl[:, 0], khl[:, 1]
        qs = sb("qs", [KR + H, 2, PAIRS, W], F32R)
        ks = sb("ks", [KR + H, 2, PAIRS, 2, W], F32R)
        vpad = sb("vpad", [P, 2, 2, H, 32])
        vlast = sb("vlast", [P, 2, P])
        bq = sb("bq", [KR, 2, 4 * P + 8], F32R)
        bk = sb("bk", [KR + H, 2, 4 * P + 8], F32R)
        mx = sb("mx", [P, 2, 2, H])
        mxl = sb("mxl", [P, 2])
        pt = sb("pt", [P, 2, H, W])
        pl = sb("pl", [P, 2, W])
        rden = sb("rden", [P, W])
        h2n = sb("h2n", [P, 2, W])
        xn2 = sb("xn2", [P, 2, W])
        stat2 = sb("stat2", [P, 2, W])
        gl = sb("gl", [P, 4, CH, E])
        oh = sb("oh", [P, 2, CH, E])
        gm = sb("gm", [P, 8, CH])
        cw = sb("cw", [P, CH, NE])
        cw2 = sb("cw2", [P, CH, E])
        cwp = sb("cwp", [P, CH, P])
        xh = sb("xh", [P, 2, W], F32R)
        xl = sb("xl", [P, 2, W], F32R)
        cwt = sb("cwt", [P, 2, W], F32R)
        h2 = sb("h2", [P, 2, W])
        gbuf = sb("gbuf", [P, NB, 2, W])
        ubuf = sb("ubuf", [P, NB, 2, W])
        tbuf = sb("tbuf", [P, NB, 2, W])
        te = sb("te", [P, NTE, 2, W])
        yo = stat2
        osb = sb("osb", [P, CH, P])
        sel_stage = te[:, :, :, :].rearrange("p c s n -> p (c s n)")[:, 0:NF * P]
        w1_stage = pt[:, :, :, :].rearrange("p c h n -> p (c h n)")[:, 0:2 * NF * P]

        slot_mem = [ctx.enter_context(nc.psum_tensor(f"slot{i}", [P, 2, 512], F32)) for i in range(NSLOT)]

        def const(name):
            a, b = CONSTS[name]
            return cst[:, a:b]

        ident = const("ident")
        par = const("par").rearrange("p (k c) -> p k c", c=NF)
        B1G, B1U, ALPHA, GSCALE, SHIFT, CLG, CLU = range(7)
        UB, HA, GHI, GLO, UHI, ULO, WSC = range(7)

        full = [sem(f"psum_full{i}") for i in range(NSLOT)]
        free = [sem(f"psum_free{i}") for i in range(NSLOT)]
        s_first, s_const, s_sel, s_w1, s_w2 = sem("first_loaded"), sem("const_loaded"), sem("sel_loaded"), sem("w1_loaded"), sem("w2_loaded")
        s_x, s_out = sem("x_loaded"), sem("out_stored")
        s_init, s_clear, s_hot = sem("constants_set"), sem("tiles_cleared"), sem("hot_rows_written")
        s_zero = sem("tiles_zeroed")
        s_seta, s_setd = sem("act_setup"), sem("dve_setup")
        names = ("zs zmin zpos zabs ef ti tm dlog wlog rmax half drel rfac gfac dec trm rar fin ed eq er efin rg rr den "
                 "term state rec es h1 rs1 rs2 qh kh vpad spill stack bq bk nm nml rden "
                 "h2n h2 xh xl cwl gtop gexp cwp cwt gclip uclip th gg te b2 ffn osb sum").split()
        S = {n: sem("r_" + n) for n in names}

        block = ctx.enter_context(nc.Block())

        def ge(eng, name, value):
            if not isinstance(value, int) or value > 0:
                eng.wait_ge(S[name] if isinstance(name, str) else name, value)

        def slot(st, name):
            return slot_mem[st.use(name)[0]]

        def take(eng, st, name):
            i, before = st.use(name)
            ge(eng, free[i], before)

        def filled(eng, st, name):
            i, before = st.use(name)
            eng.wait_ge(full[i], before + 1)

        def released(eng, st, name):
            i, before = st.use(name)
            eng.wait_ge(free[i], before + 1)

        def fill(instr, st, name):
            instr.then_inc(full[st.use(name)[0]], 1)

        def release(instr, st, name):
            instr.then_inc(free[st.use(name)[0]], 1)

        def run(eng, pieces, unrolled=False):
            def step(kind, i):
                st = Step(kind, i)
                for stage, piece, *numbers in st.plan:
                    if piece in pieces:
                        pieces[piece](st, st.unit(stage), *numbers)

            step(-2, -2)
            step(-1, -1)
            if unrolled:
                for i in range(LOOPED):
                    step(0, i)
            else:
                with eng.Fori(0, LOOPED) as i:
                    step(0, i)
            step(LOOPED, LOOPED)
            step(LOOPED + 1, LOOPED + 1)

        x_units = x_in.rearrange("p (u s t) -> u p s t", u=UNITS, s=2)
        out_units = out.rearrange("(s u) n c -> u s n c", s=2)
        NSTACK = 9
        SMALL = 19
        SETUP = 10
        INIT = 4
        ZEROED = 7

        @block.sync
        def _(sp):
            sp.dma_start(xt[:, :, :], x_units[0]).then_inc(s_x, 16)
            sp.dma_start(cst[:, 0:NFIRST], consts_in[:, 0:NFIRST]).then_inc(s_first, 16)
            sp.dma_start(cst[:, NFIRST:], consts_in[:, NFIRST:]).then_inc(s_const, 16)
            sp.dma_start(w1_stage, w1_in).then_inc(s_w1, 16)
            sp.dma_start(sel_stage, sel_in).then_inc(s_sel, 16)
            sp.dma_start(w2[:, :, :], w2_in.rearrange("p (c n) -> p c n", n=P)).then_inc(s_w2, 16)

            def token(st, u, k):
                if k == 1 and u + 1 < UNITS:
                    released(sp, st, ("zh",))
                    sp.dma_start(xt[:, :, :], x_units[u + 1]).then_inc(s_x, 16)

            def project(st, u):
                for k, name in enumerate(("q", "k")):
                    ge(sp, name + "h", u + 1)
                    released(sp, st, (name,))
                    sp.dma_start(spill[u][2 * k:2 * k + 2].rearrange("k p s n -> p k s n"),
                                 (qhl, khl)[k][:, :, :, :].bitcast(F32)).then_inc(S["spill"], 16)
                if st.kind == -2:
                    sp.wait_ge(s_zero, 1)
                ge(sp, "h2n", 2 * u)
                sp.wait_ge(S["spill"], 32 * (u + 1))
                for r, src in enumerate((0, 1, 0)):
                    sp.dma_start(qs[32 * r:32 * r + 32, :, :, :].bitcast(F32),
                                 spill[u][src].rearrange("(t p) s n -> p s t n", p=32)).then_inc(S["stack"], 16)
                for r, src in enumerate((2, 2, 3)):
                    by_head = spill[u][src].rearrange("(t i p) s n -> i p s t n", i=2, p=16)
                    for i in range(2):
                        sp.dma_start(ks[32 * r + 16 * i:32 * r + 16 * i + 16, :, :, i, :].bitcast(F32), by_head[i])\
                          .then_inc(S["stack"], 16)

            def store(st, u):
                released(sp, st, ("out",))
                for s in range(2):
                    dst = out_units[u]
                    sp.dma_start(dst[s, 0:256, :].rearrange("(c p) n -> p c n", p=P), osb[:, 2 * s:2 * s + 2, :])\
                      .then_inc(s_out, 16)
                    sp.dma_start(dst[s, 256:257, :], osb[ROWS[s]:ROWS[s] + 1, 4, :]).then_inc(s_out, 16)

            run(sp, {"token": token, "project": project, "out": store}, unrolled=True)
            sp.wait_ge(s_out, 64 * UNITS + 1)

        @block.gpsimd
        def _(pool):
            pool.memset(one[:, :], 1.0).then_inc(s_init, 1)
            pool.memset(eps[:, :], EPS).then_inc(s_init, 1)
            pool.memset(rmax[:, :, 0:1], 0.0).then_inc(s_init, 1)
            pool.memset(h1[:, :, :], 0.5).then_inc(s_init, 1)
            pool.wait_ge(s_init, 4)
            pool.memset(credit[:, :], 1.0).then_inc(s_out, 1)
            pool.wait_ge(s_out, 1)
            pool.memset(vpad[:, :, :, :, :], 0.0).then_inc(s_clear, 1)

            g = nc.gpsimd

            def token(st, u, k):
                if k == 2:
                    ge(pool, "zmin", u + 1)
                    g.tensor_tensor(dlog, zmin[:, 1, :, :], zmin[:, 0, :, :], ALU.subtract).then_inc(S["dlog"], 1)
                    ge(pool, "ef", u + 1)
                    ge(pool, "dlog", u + 1)
                    g.tensor_tensor(wlog, dlog, zmin[:, 2, :, :], ALU.add).then_inc(S["wlog"], 1)
                    g.tensor_scalar(half[:, :, :], zabs[:, 0, :, :], 1.0, 0.5, ALU.add, ALU.mult).then_inc(S["half"], 1)
                elif k == 4:
                    ge(pool, "rmax", 2 * u + 2)
                    ge(pool, "es", u)
                    g.tensor_tensor(earg[:, 0, :, :], rmax[:, :, 0:T], rmax[:, :, 1:N], ALU.subtract).then_inc(S["dec"], 1)
                    g.tensor_tensor(earg[:, 1, :, :], wlog, rmax[:, :, 1:N], ALU.subtract).then_inc(S["trm"], 1)
                    ge(pool, "drel", u + 1)
                    g.tensor_tensor(earg[:, 2, :, :], dlog, drel[:, :, :], ALU.subtract).then_inc(S["rar"], 1)
                    g.tensor_tensor(fexp[:, :, :], rmax[:, :, 1:N], drel[:, :, :], ALU.subtract).then_inc(S["fin"], 1)
                elif k == 6:
                    ge(pool, "rfac", u + 1)
                    ge(pool, "gfac", u + 1)
                    g.tensor_tensor(gate[:, :, :], gate[:, :, :], half[:, :, :], ALU.mult).then_inc(S["rg"], 1)
                    ge(pool, "er", u + 1)
                    g.tensor_tensor(earg[:, 2, :, :], earg[:, 2, :, :], half[:, :, :], ALU.mult).then_inc(S["rr"], 1)
                    ge(pool, "rr", u + 1)
                    ge(pool, "eq", u + 1)
                    g.tensor_tensor(earg[:, 2, :, :], earg[:, 2, :, :], drel[:, :, :], ALU.add).then_inc(S["den"], 1)

            def cw_(st, u, c):
                ge(pool, "gg", NF * u + c + 1)
                released(pool, st, ("cw", c))
                if c >= NTE:
                    burst = next(b for b, (_, end) in enumerate(BURSTS) if end > c - NTE)
                    filled(pool, st, ("down", burst))
                g.tensor_tensor(te[:, c % NTE, :, :], tbuf[:, c % NB, :, :], ubuf[:, c % NB, :, :], ALU.mult)\
                    .then_inc(S["te"], 1)

            pool.wait_ge(s_clear, 1)
            run(pool, {"token": token, "cw": cw_})

        @block.scalar
        def _(act):
            a = nc.scalar.activation

            def tables(number):
                nc.scalar.add_instruction(mybir.InstLoadActFuncSet(
                    name=nc.get_next_instruction_name(), act_func_set_id=number, ins=[], outs=[]))

            def token(st, u, k):
                flat = lambda ap: ap.rearrange("p s t -> p (s t)")
                btok = const("btok")
                if k == 0:
                    ge(act, "h1", u)
                    for j, name in enumerate(("zf", "zi", "zh")):
                        filled(act, st, (name,))
                        release(a(flat(zs[:, j, :, :]), slot(st, (name,))[:, 0, :], ACT.Identity, bias=btok[:, j:j + 1]),
                                st, (name,))
                elif k == 1:
                    released(act, st, ("zi",))
                    a(zabs[:, :, :, :], zs[:, 0:2, :, :], ACT.Abs).then_inc(S["zabs"], 1)
                elif k == 2:
                    ge(act, "zabs", u + 1)
                    a(zabs[:, 0, :, :], zabs[:, 0, :, :], ACT.Exp, scale=-1.0).then_inc(S["ef"], 1)
                    a(zabs[:, 1, :, :], zabs[:, 1, :, :], ACT.Tanh, scale=0.5).then_inc(S["ti"], 1)
                    ge(act, "zmin", u + 1)
                    a(gate[:, :, :], zmin[:, 2, :, :], ACT.Tanh, scale=0.5).then_inc(S["tm"], 1)
                elif k == 3:
                    ge(act, "dlog", u + 1)
                    a(drel[:, :, :], dlog, ACT.Relu).then_inc(S["drel"], 1)
                elif k == 5:
                    ge(act, "dec", u + 1)
                    ge(act, "trm", u + 1)
                    a(earg[:, 0:2, :, :], earg[:, 0:2, :, :], ACT.Exp).then_inc(S["ed"], 1)
                    ge(act, "rar", u + 1)
                    a(earg[:, 2, :, :], earg[:, 2, :, :], ACT.Exp).then_inc(S["er"], 1)
                    ge(act, "fin", u + 1)
                    a(drel[:, :, :], drel[:, :, :], ACT.Exp, scale=-1.0).then_inc(S["eq"], 1)
                    a(fexp[:, :, :], fexp[:, :, :], ACT.Exp).then_inc(S["efin"], 1)

            def center(st, u, which):
                stat = (stat1, stat2)[which - 1]
                filled(act, st, ("cent", which))
                release(a(stat[:, :, :], slot(st, ("cent", which))[:, :, 0:W], ACT.Square), st, ("cent", which))

            def variance(st, u, which):
                stat = (stat1, stat2)[which - 1]
                if which == 2 or st.kind == -2:
                    tables(SET_EXP_LN)
                filled(act, st, ("var", which))
                release(a(stat[:, :, :], slot(st, ("var", which))[:, :, 0:W], ACT.Ln, bias=eps[:, :]), st, ("var", which))
                released(act, st, ("var", which))
                a(stat[:, :, :], stat[:, :, :], ACT.Exp, scale=-0.5).then_inc(S[f"rs{which}"], 1)
                if st.kind == -2:
                    clamps()
                if which == 1 or st.kind == LOOPED:
                    tables(SET_EXP_TANH)

            def project(st, u):
                filled(act, st, ("q",))
                a(qh[:, :, :], slot(st, ("q",))[:, :, 0:W], ACT.Copy).then_inc(S["qh"], 1)
                filled(act, st, ("k",))
                a(kh[:, :, :], slot(st, ("k",))[:, :, 0:W], ACT.Copy).then_inc(S["kh"], 1)
                if st.kind == -2:
                    act.wait_ge(s_clear, 1)
                ge(act, "h2n", 2 * u)
                for s in range(2):
                    dst = vpad[:, s, :, :, :].rearrange("p c (j i) x -> p (c j) (i x)", i=2)
                    filled(act, st, (f"v{s}",))
                    src = slot(st, (f"v{s}",))[:, 0, 0:256].rearrange("p (cj i x) -> p cj i x", i=2, x=DH)
                    for i in range(2):
                        a(dst[:, :, 48 * i:48 * i + DH], src[:, :, i, :], ACT.Copy).then_inc(S["vpad"], 1)
                if st.kind == -2:
                    act.wait_ge(s_w1, 16)
                    a(w1h[:, :, :, :].rearrange("p k c n -> p (k c n)"), w1_stage, ACT.Copy).then_inc(s_seta, 1)
                    act.wait_ge(s_sel, 16)
                    a(sel[:, :, :].rearrange("p c n -> p (c n)"), sel_stage, ACT.Copy).then_inc(s_seta, 1)

            def mlast(st, u, s):
                name = ("mlast", s)
                filled(act, st, name)
                a(qs[KR:KR + H, s, :, 0:256], slot(st, name)[KR:KR + H, 1:2, 0:256].to_broadcast([H, PAIRS, 256]),
                  ACT.Copy, scale=-1.0).then_inc(S["nm"], 1)

            def plast(st, u, s):
                name = ("plast", s)
                filled(act, st, name)
                release(a(pl[:, s, :], slot(st, name)[:, 0, 0:W], ACT.Exp, scale=SCORE_SCALE), st, name)

            def st_(st, u, s, c, t):
                name = ("st", s, c, t)
                if (c, t) == (0, 0):
                    if s:
                        filled(act, st, ("pv", 0))
                    elif st.kind == -1:
                        act.wait_ge(s_setd, SETUP)
                    else:
                        ge(act, "h2n", 2 * u)
                filled(act, st, name)
                release(a(pt[:, c, 2 * t:2 * t + 2, :], slot(st, name)[:, :, 0:W], ACT.Exp, scale=SCORE_SCALE), st, name)

            def split(st, u):
                released(act, st, ("xc", 2))
                if st.kind != -1:
                    filled(act, st, ("u", NF - 1))
                a(xh[:, :, :], xn2[:, :, :], ACT.Copy).then_inc(S["xh"], 1)

            def route(st, u, k):
                if k == ROUTE - 2:
                    ge(act, "gtop", u + 1)
                    a(gm[:, 5, :], gm[:, 4, :], ACT.Exp).then_inc(S["gexp"], 1)

            def cwt_(st, u):
                filled(act, st, ("cwt",))
                a(cwt[:, :, 0:256], slot(st, ("cwt",))[:, 0, :].rearrange("p (s t) -> p s t", s=2), ACT.Copy)
                release(a(cwt[:, :, 256], slot(st, ("cwt",))[:, 1, ROWS[0]:ROWS[1] + 1:ROWS[1] - ROWS[0]], ACT.Copy),
                        st, ("cwt",))

            def keep(st, u):
                if st.kind != -1:
                    released(act, st, ("down", len(BURSTS) - 1))
                a(h2[:, :, :], h2n[:, :, :], ACT.Copy).then_inc(S["h2"], 1)

            def gate_half(st, u, c):
                filled(act, st, ("g", c))
                if c >= NB:
                    ge(act, "gg", NF * u + c + 1 - NB)
                release(a(gbuf[:, c % NB, :, :], slot(st, ("g", c))[:, :, 0:W], ACT.Identity, bias=par[:, B1G, c:c + 1]),
                        st, ("g", c))
                if c:
                    tanh(u, c - 1)

            def up_half(st, u, c):
                filled(act, st, ("u", c))
                if c >= NB:
                    ge(act, "te", NF * u + c + 1 - NB)
                release(a(ubuf[:, c % NB, :, :], slot(st, ("u", c))[:, :, 0:W], ACT.Identity, bias=fpar[:, UB, c:c + 1]),
                        st, ("u", c))
                if c == NF - 1:
                    tanh(u, c)

            def tanh(u, c):
                ge(act, "gclip", NF * u + c + 1)
                if c >= NB:
                    ge(act, "te", NF * u + c + 1 - NB)
                a(tbuf[:, c % NB, :, :], gbuf[:, c % NB, :, :], ACT.Tanh, scale=fpar[:, HA, c:c + 1])\
                    .then_inc(S["th"], 1)

            def out_(st, u):
                filled(act, st, ("out",))
                ge(act, s_out, 64 * u + 1)
                for k in range(CH):
                    last = a(osb[:, k, :].rearrange("p (d h) -> p h d", h=H),
                             slot(st, ("out",))[:, k // 4, (k % 4) * P:(k % 4 + 1) * P].rearrange("p (h d) -> p h d", h=H),
                             ACT.Copy)
                release(last, st, ("out",))

            def clamps():
                raw = par[:, CLG:CLU + 1, :].rearrange("p k c -> p (k c)")
                act.wait_ge(s_const, 16)
                a(clt[:, 0, :], raw, ACT.Abs).then_inc(s_seta, 1)
                act.wait_ge(s_seta, 1)
                a(clt[:, 1, :], clt[:, 0, :], ACT.Exp, scale=-1.0).then_inc(s_seta, 1)
                act.wait_ge(s_seta, 2)
                a(clt[:, 2, :], clt[:, 1, :], ACT.Ln, bias=one[:, :]).then_inc(s_seta, 1)

            tables(SET_EXP_TANH)
            act.wait_ge(s_init, INIT)
            act.wait_ge(s_first, 16)
            run(act, {"token": token, "center": center, "variance": variance, "project": project, "mlast": mlast,
                      "plast": plast, "st": st_, "split": split, "route": route, "cwt": cwt_, "keep": keep,
                      "g": gate_half, "u": up_half, "out": out_})

        @block.vector
        def _(dve):
            v = nc.vector

            def token(st, u, k):
                if k == 1:
                    released(dve, st, ("zh",))
                    ge(dve, "wlog", u)
                    v.tensor_scalar(zmin[:, :, :, :], zs[:, :, :, :], 0.0, None, ALU.min).then_inc(S["zmin"], 1)
                    v.tensor_scalar(zpos[:, :, :], zs[:, 2, :, :], 0.0, 0.5, ALU.max, ALU.add).then_inc(S["zpos"], 1)
                elif k == 3:
                    ge(dve, "wlog", u + 1)
                    for s in range(2):
                        v.tensor_tensor_scan(rmax[:, s, 1:N], wlog[:, s, :], wlog[:, s, :], 0.0, ALU.max, ALU.max)\
                            .then_inc(S["rmax"], 1)
                elif k == 4:
                    ge(dve, "tm", u + 1)
                    ge(dve, "zpos", u + 1)
                    v.scalar_tensor_tensor(gate[:, :, :], gate[:, :, :], -0.5, zpos[:, :, :], ALU.mult, ALU.add)\
                        .then_inc(S["gfac"], 1)
                    ge(dve, "ti", u + 1)
                    ge(dve, "half", u + 1)
                    v.scalar_tensor_tensor(half[:, :, :], zabs[:, 1, :, :], 1.0, half[:, :, :], ALU.add, ALU.mult)\
                        .then_inc(S["rfac"], 1)
                elif k == 7:
                    ge(dve, "rg", u + 1)
                    ge(dve, "ed", u + 1)
                    v.tensor_tensor(gate[:, :, :], gate[:, :, :], earg[:, 1, :, :], ALU.mult).then_inc(S["term"], 1)
                    ge(dve, "den", u + 1)
                    v.reciprocal(earg[:, 2, 0, :], earg[:, 2, 0, :]).then_inc(S["rec"], 1)
                    ge(dve, "term", u + 1)
                    for s in range(2):
                        v.tensor_tensor_scan(state[:, s, :], earg[:, 0, s, :], gate[:, s, :], 0.5, ALU.mult, ALU.add)\
                            .then_inc(S["state"], 1)
                elif k == 8:
                    v.reciprocal(earg[:, 2, 1, :], earg[:, 2, 1, :]).then_inc(S["rec"], 1)
                    ge(dve, "state", 2 * u + 2)
                    ge(dve, "efin", u + 1)
                    v.tensor_tensor(state[:, :, :], fexp[:, :, :], state[:, :, :], ALU.mult).then_inc(S["es"], 1)
                elif k == 9:
                    ge(dve, "es", u + 1)
                    ge(dve, "rec", 2 * u + 2)
                    ge(dve, "h2n", 2 * u)
                    v.tensor_tensor(h1[:, :, 1:N], earg[:, 2, :, :], state[:, :, :], ALU.mult).then_inc(S["h1"], 1)

            def scale(st, u, which):
                name = ("xc", which)
                ge(dve, f"rs{which}", u + 1)
                filled(dve, st, name)
                xn, stat = ((xn1, stat1), (xn2, stat2))[which - 1]
                release(v.tensor_tensor(xn[:, :, :], slot(st, name)[:, :, 0:W], stat[:, :, :], ALU.mult), st, name)

            def project(st, u):
                if st.kind == -2:
                    dve.wait_ge(s_const, 16)
                for name, hi, lo in (("q", qh, ql), ("k", kh, kl)):
                    filled(dve, st, (name,))
                    ge(dve, name + "h", u + 1)
                    release(v.tensor_tensor(lo[:, :, :], slot(st, (name,))[:, :, 0:W], hi[:, :, :].bitcast(F32),
                                            ALU.subtract), st, (name,))
                for s in range(2):
                    name = (f"v{s}",)
                    filled(dve, st, name)
                    ge(dve, "vpad", 4 * u + 2 * s + 2)
                    release(v.tensor_tensor(vlast[:, s, :], slot(st, name)[:, 0, 256:384], const("mask8"), ALU.mult),
                            st, name)
                if st.kind == -2:
                    v.tensor_copy(ks[KR:KR + H, :, :, :, :].rearrange("p s t i n -> p s (t i) n"),
                                  const("hot")[KR:KR + H, :].unsqueeze(1).unsqueeze(3).to_broadcast([H, 2, H, W]))\
                     .then_inc(s_hot, 1)
                    parameters()

            def last_position(u):
                ge(dve, "stack", 16 * NSTACK * (u + 1))
                for s in range(2):
                    dq = bq[:, s, :].rearrange("p (t x) -> p t x", x=130)[:, :, KR:KR + 2]
                    v.tensor_tensor(dq, qs[0:KR, s, :, 256:257].bitcast(F32).to_broadcast([KR, PAIRS, 2]),
                                    const("maskp")[0:KR, :].unsqueeze(1).to_broadcast([KR, PAIRS, 2]), ALU.mult)\
                        .then_inc(S["bq"], 1)
                    dk = bk[:, s, :].rearrange("p (t x) -> p t x", x=130)[:, :, 0:2]
                    v.tensor_copy(dk, ks[:, s, :, :, 256].bitcast(F32)).then_inc(S["bk"], 1)

            def max_(st, u, s, c, t):
                if (s, c, t) == (0, 0, 0):
                    last_position(u)
                name = ("max", s, c, t)
                filled(dve, st, name)
                release(v.tensor_reduce(mx[:, s, c, 2 * t:2 * t + 2], slot(st, name)[:, :, 0:N], AX_X, ALU.max), st, name)

            def mtop(st, u, s):
                name = ("mlast", s)
                filled(dve, st, name)
                ge(dve, "nm", 2 * u + s + 1)
                release(v.tensor_reduce(mxl[KR:KR + H, s:s + 1], slot(st, name)[KR:KR + H, 0, 0:N], AX_X, ALU.max), st, name)
                released(dve, st, name)
                v.tensor_scalar(qs[KR:KR + H, s, :, 256], mxl[KR:KR + H, s:s + 1].to_broadcast([H, PAIRS]), -1.0, None,
                                ALU.mult).then_inc(S["nml"], 1)

            def norm(st, u, s):
                name = ("pv", s)
                filled(dve, st, name)
                ge(dve, "h2n", 2 * u + s)
                v.reciprocal(rden[:, :], slot(st, name)[:, 1, 0:W]).then_inc(S["rden"], 1)
                ge(dve, "rden", 2 * u + s + 1)
                release(v.tensor_tensor(rden[:, :], slot(st, name)[:, 0, 0:W], rden[:, :], ALU.mult), st, name)
                released(dve, st, name)
                v.tensor_tensor(h2n[:, s, 0:N], rden[:, 0:N], h1[:, s, 0:N], ALU.add).then_inc(S["h2n"], 1)

            def wide(ap):
                return ap.unsqueeze(2).to_broadcast([P, CH, E])

            def gate_(st, u):
                filled(dve, st, ("gate",))
                release(v.tensor_tensor(gl[:, 0, :, :],
                                        slot(st, ("gate",))[:, 0, 0:CH * E].rearrange("p (k e) -> p k e", e=E),
                                        const("gate_b").unsqueeze(1).to_broadcast([P, CH, E]), ALU.add), st, ("gate",))

            def route(st, u, k):
                after = lambda n: ge(dve, "cwl", u * SMALL + n)
                done = lambda ins: ins.then_inc(S["cwl"], 1)
                rank = const("rank").unsqueeze(1).to_broadcast([P, CH, E])
                if k in (0, 1, 2):
                    r, n = ((0, 0), (0, 3), (1, 6))[k]
                    if k == 0:
                        released(dve, st, ("gate",))
                    else:
                        after(n)
                if k in (0, 2):
                    done(v.tensor_reduce(gm[:, r, :], gl[:, r, :, :], AX_X, ALU.max))
                    after(n + 1)
                    done(v.tensor_tensor(gl[:, 2, :, :], gl[:, r, :, :], wide(gm[:, r, :]), ALU.is_equal))
                    after(n + 2)
                    done(v.tensor_tensor(gl[:, 3, :, :], gl[:, 2, :, :], rank, ALU.mult))
                elif k == 1:
                    done(v.tensor_reduce(gm[:, 2, :], gl[:, 3, :, :], AX_X, ALU.max))
                    after(4)
                    done(v.tensor_tensor(oh[:, 0, :, :], rank, wide(gm[:, 2, :]), ALU.is_equal))
                    after(5)
                    done(v.scalar_tensor_tensor(gl[:, 1, :, :], oh[:, 0, :, :], -1e30, gl[:, 0, :, :], ALU.mult, ALU.add))
                elif k == 3:
                    v.tensor_tensor(gm[:, 4, :], gm[:, 1, :], gm[:, 0, :], ALU.subtract).then_inc(S["gtop"], 1)
                    after(9)
                    done(v.tensor_reduce(gm[:, 3, :], gl[:, 3, :, :], AX_X, ALU.max))
                    after(10)
                    done(v.tensor_tensor(oh[:, 1, :, :], rank, wide(gm[:, 3, :]), ALU.is_equal))
                elif k == 4:
                    ge(dve, "gexp", u + 1)
                    done(v.tensor_scalar(gm[:, 6, :], gm[:, 5, :], 1.0, None, ALU.add))
                    after(12)
                    done(v.reciprocal(gm[:, 7, :], gm[:, 6, :]))
                    after(13)
                    done(v.tensor_tensor(gm[:, 6, :], gm[:, 5, :], gm[:, 7, :], ALU.mult))
                    done(v.tensor_tensor(cw[:, :, 0:E], oh[:, 0, :, :], wide(gm[:, 7, :]), ALU.mult))
                    after(14)
                    done(v.tensor_tensor(cw2[:, :, :], oh[:, 1, :, :], wide(gm[:, 6, :]), ALU.mult))
                    after(16)
                    done(v.tensor_tensor(cw[:, :, 0:E], cw[:, :, 0:E], cw2[:, :, :], ALU.add))
                    after(17)
                    done(v.tensor_copy(cwp[:, :, 0:NE].bitcast(F32R), cw[:, :, :]))
                    after(18)
                    done(v.tensor_tensor(cwp[:, :, 32:32 + NE], cw[:, :, :], cwp[:, :, 0:NE], ALU.subtract))

            def split(st, u):
                ge(dve, "xh", u + 1)
                v.tensor_tensor(xl[:, :, :], xn2[:, :, :], xh[:, :, :].bitcast(F32), ALU.subtract).then_inc(S["xl"], 1)

            def clip_gate(st, u, c):
                released(dve, st, ("g", c))
                p = c % NB
                v.tensor_scalar(gbuf[:, p, :, :], gbuf[:, p, :, :], fpar[:, GHI, c:c + 1], fpar[:, GLO, c:c + 1],
                                ALU.min, ALU.max).then_inc(S["gclip"], 1)

            def clip_up(st, u, c):
                released(dve, st, ("u", c))
                p = c % NB
                v.tensor_scalar(ubuf[:, p, :, :], ubuf[:, p, :, :], fpar[:, UHI, c:c + 1], fpar[:, ULO, c:c + 1],
                                ALU.min, ALU.max).then_inc(S["uclip"], 1)

            def gated(st, u, c):
                p = c % NB
                ge(dve, "th", NF * u + c + 1)
                v.scalar_tensor_tensor(tbuf[:, p, :, :], tbuf[:, p, :, :], 1.0, gbuf[:, p, :, :], ALU.add, ALU.mult)\
                    .then_inc(S["gg"], 1)

            def cw_(st, u, c):
                p = c % NB
                filled(dve, st, ("cw", c))
                ge(dve, "uclip", NF * u + c + 1)
                release(v.tensor_tensor(ubuf[:, p, :, :], slot(st, ("cw", c))[:, :, 0:W], ubuf[:, p, :, :], ALU.mult),
                        st, ("cw", c))

            def add(st, u, b):
                name = ("down", b)
                filled(dve, st, name)
                if b == 0:
                    ge(dve, "h2", u + 1)
                else:
                    released(dve, st, ("down", b - 1))
                last = b == len(BURSTS) - 1
                release(v.tensor_tensor((yo if last else h2)[:, :, :], slot(st, name)[:, :, 0:W], h2[:, :, :], ALU.add),
                        st, name)

            steps = [0]

            def then(ins):
                steps[0] += 1
                ins.then_inc(s_setd, 1)
                dve.wait_ge(s_setd, steps[0])

            def parameters():
                raw = par[:, CLG:CLU + 1, :].rearrange("p k c -> p (k c)")
                dve.wait_ge(s_seta, 3)
                then(v.scalar_tensor_tensor(clt[:, 0, :], raw, 0.0, clt[:, 2, :], ALU.max, ALU.add))
                cg, cu = clt[:, 0, 0:NF], clt[:, 0, NF:2 * NF]
                then(v.tensor_copy(fpar[:, GHI, :], cg))
                then(v.tensor_scalar(fpar[:, GLO, :], cg, -1.0, None, ALU.mult))
                then(v.tensor_tensor(fpar[:, UHI, :], par[:, SHIFT, :], cu, ALU.add))
                then(v.tensor_tensor(fpar[:, ULO, :], par[:, SHIFT, :], cu, ALU.subtract))
                then(v.tensor_tensor(fpar[:, UB, :], par[:, B1U, :], par[:, SHIFT, :], ALU.add))
                then(v.tensor_scalar(fpar[:, HA, :], par[:, ALPHA, :], 0.5, None, ALU.mult))
                then(v.tensor_scalar(fpar[:, WSC, :], par[:, GSCALE, :], 0.5, None, ALU.mult))
                dve.wait_ge(s_w2, 16)
                then(v.tensor_tensor(w2[:, :, :], w2[:, :, :], fpar[:, WSC, :].unsqueeze(2).to_broadcast([P, NF, P]),
                                     ALU.mult))
                dve.wait_ge(s_seta, 4)
                then(v.tensor_tensor(w1l[:, :, :, :].rearrange("p k c n -> p (k c n)"), w1_stage,
                                     w1h[:, :, :, :].rearrange("p k c n -> p (k c n)").bitcast(F32), ALU.subtract))

            for tile in (ks[0:KR, :, :, :, :], qs[KR:KR + H, :, :, N:W], bq[:, :, :], bk[:, :, :], cwt[:, :, N:W]):
                v.memset(tile.bitcast(F32), 0.0).then_inc(s_zero, 1)
            v.memset(h2n[:, :, N:W], 0.5).then_inc(s_zero, 1)
            v.memset(cwp[:, :, :], 0.0).then_inc(s_zero, 1)
            v.memset(cw[:, :, E:NE], 1.0)
            dve.wait_ge(s_first, 16)
            dve.wait_ge(s_init, INIT)
            run(dve, {"token": token, "scale": scale, "project": project, "max": max_, "mtop": mtop, "norm": norm,
                      "gate": gate_, "route": route, "split": split, "clip_gate": clip_gate, "clip_up": clip_up,
                      "gated": gated, "cw": cw_, "add": add})

        @block.tensor
        def _(pe):
            def mm(out_, lhsT, rhs, start=True, stop=True, **k):
                return nc.tensor.matmul(out_, lhsT, rhs, start=start, stop=stop, **k)

            def token(st, u, k):
                if k:
                    return
                pe.wait_ge(s_x, 16 * (u + 1))
                wtok = const("wtok").rearrange("p (k n) -> p k n", n=P)
                xall = xt[:, :, :].rearrange("p s t -> p (s t)")
                for j, name in enumerate(("zf", "zi", "zh")):
                    take(pe, st, (name,))
                    fill(mm(slot(st, (name,))[:, 0, :], wtok[:, j, :], xall), st, (name,))

            def centered(st, u, name, which):
                take(pe, st, name)
                ge(pe, ("h1", "h2n")[which - 1], (u + 1, 2 * u + 2)[which - 1])
                for s in range(2):
                    last = mm(slot(st, name)[:, s, 0:W], const("cmat"), (h1, h2n)[which - 1][:, s, :])
                fill(last, st, name)

            def center(st, u, which):
                centered(st, u, ("cent", which), which)

            def scale(st, u, which):
                centered(st, u, ("xc", which), which)

            def variance(st, u, which):
                name = ("var", which)
                take(pe, st, name)
                released(pe, st, ("cent", which))
                for s in range(2):
                    last = mm(slot(st, name)[:, s, 0:W], const("omat"), (stat1, stat2)[which - 1][:, s, :])
                fill(last, st, name)

            def project(st, u):
                if st.kind == -2:
                    pe.wait_ge(s_const, 16)
                released(pe, st, ("xc", 1))
                for name in ("q", "k"):
                    take(pe, st, (name,))
                    for s in range(2):
                        last = mm(slot(st, (name,))[:, s, 0:W], const("w" + name), xn1[:, s, :])
                    fill(last, st, (name,))
                for s in range(2):
                    name = (f"v{s}",)
                    take(pe, st, name)
                    for c in range(2):
                        mm(slot(st, name)[:, 0, c * P:(c + 1) * P], xn1[:, s, c * P:(c + 1) * P], const("wv"))
                    fill(mm(slot(st, name)[:, 0, 256:384], xn1[:, s, 256:257].to_broadcast([P, P]), const("wv")), st, name)

            def max_(st, u, s, c, t):
                name = ("max", s, c, t)
                if (s, c, t) == (0, 0, 0):
                    ge(pe, "stack", 16 * NSTACK * (u + 1))
                    if st.kind == -1:
                        pe.wait_ge(s_zero, ZEROED)
                        pe.wait_ge(s_hot, 1)
                take(pe, st, name)
                for i in range(2):
                    last = mm(slot(st, name)[:, i, 0:W], qs[0:KR, s, t, c * P:(c + 1) * P], ks[0:KR, 1 - s, t, i, :])
                fill(last, st, name)

            def mlast(st, u, s):
                name = ("mlast", s)
                take(pe, st, name)
                ge(pe, "bq", 2 * u + 2)
                for k in range(H):
                    t, i = divmod(k, 2)
                    mm(slot(st, name)[:, 0, 0:W], bq[:, s, t * P:(t + 1) * P], ks[0:KR, 1 - s, t, i, :],
                       start=(k == 0), stop=(k == H - 1))
                released(pe, st, ("max", s, 1, PAIRS - 1))
                for c in range(2):
                    last = mm(slot(st, name)[KR:KR + H, 1, c * P:(c + 1) * P], mx[:, s, c, :], ident)
                fill(last, st, name)

            def plast(st, u, s):
                name = ("plast", s)
                take(pe, st, name)
                ge(pe, "nm", 2 * u + s + 1)
                ge(pe, "nml", 2 * u + s + 1)
                ge(pe, "bk", 2 * u + 2)
                for t in range(PAIRS):
                    last = mm(slot(st, name)[:, 0, 0:W], bk[:, 1 - s, t * P:(t + 1) * P], qs[:, s, t, :],
                              start=(t == 0), stop=(t == PAIRS - 1))
                fill(last, st, name)

            def st_(st, u, s, c, t):
                name = ("st", s, c, t)
                take(pe, st, name)
                for i in range(2):
                    last = mm(slot(st, name)[:, i, 0:W], ks[:, 1 - s, t, i, c * P:(c + 1) * P], qs[:, s, t, :])
                fill(last, st, name)

            def pv(st, u, s):
                name = ("pv", s)
                take(pe, st, name)
                released(pe, st, ("plast", s))
                ge(pe, "vpad", 4 * u + 4)
                o = slot(st, name)
                mm(o[:, 0, 0:W], vlast[:, 1 - s, :], pl[:, s, :], stop=False)
                mm(o[:, 1, 0:W], const("mask8"), pl[:, s, :], stop=False)
                ones32 = const("ones32")
                for c in range(2):
                    released(pe, st, ("st", s, c, PAIRS - 1))
                    for i in range(2):
                        for bank in range(2):
                            for t in range(PAIRS):
                                lhsT = ones32[:, 32 * i:32 * i + 32] if bank else vpad[:, 1 - s, c, 2 * t + i, :]
                                last = mm(o[32 * t:32 * t + 32, bank, 0:W], lhsT, pt[:, c, 2 * t + i, :],
                                          start=False, stop=(c == 1 and i == 1))
                fill(last, st, name)

            def gate_(st, u):
                name = ("gate",)
                released(pe, st, ("xc", 2))
                take(pe, st, name)
                for k in range(CH):
                    s, c = divmod(k, 2)
                    lhsT = (xn2[:, s, c * P:(c + 1) * P] if k < 4
                            else xn2[:, :, :].rearrange("p s t -> p (s t)")[:, LAST])
                    last = mm(slot(st, name)[:, 0, k * E:(k + 1) * E], lhsT, const("gate_w"))
                fill(last, st, name)

            def cwt_(st, u):
                name = ("cwt",)
                take(pe, st, name)
                ge(pe, "cwl", SMALL * (u + 1))
                for k in range(CH):
                    last = nc.tensor.transpose(slot(st, name)[:, k // 4, (k % 4) * P:(k % 4 + 1) * P], cwp[:, k, :], ident)
                fill(last, st, name)

            def half_(st, u, c, k):
                name = ("gu"[k], c)
                if (c, k) == (0, 0):
                    ge(pe, "xl", u + 1)
                    if st.kind == 0:
                        pe.wait_ge(s_setd, SETUP)
                take(pe, st, name)
                for s in range(2):
                    o = slot(st, name)[:, s, 0:W]
                    mm(o, w1h[:, k, c, :], xh[:, s, :], stop=False)
                    mm(o, w1h[:, k, c, :], xl[:, s, :], start=False, stop=False)
                    last = mm(o, w1l[:, k, c, :], xh[:, s, :], start=False)
                fill(last, st, name)

            def gate_half(st, u, c):
                half_(st, u, c, 0)

            def up_half(st, u, c):
                half_(st, u, c, 1)

            def cw_(st, u, c):
                name = ("cw", c)
                take(pe, st, name)
                if c == 0:
                    pe.wait_ge(s_seta, 5)
                    ge(pe, "h2", u + 1)
                for s in range(2):
                    last = mm(slot(st, name)[:, s, 0:W], sel[:, c, :], cwt[:, s, :])
                fill(last, st, name)

            def down(st, u, b):
                name = ("down", b)
                take(pe, st, name)
                begin, end = BURSTS[b]
                if b == 0:
                    for s in range(2):
                        mm(slot(st, name)[:, s, 0:W], const("b2"), cwt[:, s, :].bitcast(F32), stop=False)
                for c in range(begin, end):
                    ge(pe, "te", NF * u + c + 1)
                    for s in range(2):
                        last = mm(slot(st, name)[:, s, 0:W], w2[:, c, :], te[:, c % NTE, s, :],
                                  start=(c == begin and b > 0), stop=(c == end - 1))
                fill(last, st, name)

            def out_(st, u):
                name = ("out",)
                take(pe, st, name)
                released(pe, st, ("down", len(BURSTS) - 1))
                for k in range(CH):
                    s, c = divmod(k, 2)
                    src = yo[:, s, c * P:(c + 1) * P] if k < 4 else yo[:, :, :].rearrange("p s t -> p (s t)")[:, LAST]
                    last = nc.tensor.transpose(slot(st, name)[:, k // 4, (k % 4) * P:(k % 4 + 1) * P], src, ident)
                fill(last, st, name)

            pe.wait_ge(s_first, 16)
            pe.wait_ge(s_init, INIT)
            run(pe, {"token": token, "center": center, "variance": variance, "scale": scale, "project": project, "max": max_,
                     "mlast": mlast, "plast": plast, "st": st_, "pv": pv, "gate": gate_, "cwt": cwt_, "g": gate_half,
                     "u": up_half, "cw": cw_, "down": down, "out": out_})


def layout(inputs):
    f = lambda n: np.asarray(inputs[n])
    j = np.arange(P)
    perm = (j % DH) * H + j // DH
    x = f("x")[[0, 4, 1, 5, 2, 6, 3, 7]].transpose(2, 0, 1).reshape(P, B * T)

    feats = NF * P
    expert_of = np.minimum(np.arange(feats) // I, NE)

    def per_feature(shared, expert):
        v = np.concatenate([np.asarray(expert).reshape(E), np.asarray(shared).reshape(1), np.zeros(1, np.float32)])
        return v[expert_of].reshape(NF, P).T

    def features(a):
        v = np.concatenate([a.reshape(-1), np.zeros(feats - NE * I, np.float32)])
        return v.reshape(NF, P).T

    b1 = np.concatenate([f("L0_ffn_expert_b1"), f("L0_ffn_shared_b1")[None]])
    ea, sa = f("L0_ffn_expert_act"), f("L0_ffn_shared_act")
    params = [features(b1[:, 0::2]), features(b1[:, 1::2])] + [per_feature(sa[k], ea[:, k]) for k in range(5)]
    w1 = np.concatenate([f("L0_ffn_expert_w1"), f("L0_ffn_shared_w1")[None]])[:, perm, :]
    w1 = w1.transpose(1, 0, 2)
    pad = np.zeros((P, feats - NE * I), np.float32)
    w1 = np.concatenate([w1[:, :, 0::2].reshape(P, -1), pad, w1[:, :, 1::2].reshape(P, -1), pad], axis=1)
    w2 = np.concatenate([f("L0_ffn_expert_w2"), f("L0_ffn_shared_w2")[None]])[:, :, perm].reshape(NE * I, D)
    w2 = np.concatenate([w2, pad.T]).reshape(NF, P, D).transpose(1, 0, 2).reshape(P, NF * D)
    b2 = np.concatenate([f("L0_ffn_expert_b2"), f("L0_ffn_shared_b2")[None]])[:, perm]
    b2s = np.zeros((P, P), np.float32)
    b2s[0:NE] = b2
    b2s[32:32 + NE] = b2

    eye = np.eye(P, dtype=np.float32)
    zero16 = np.zeros((P, DH), np.float32)
    one16 = np.ones((P, DH), np.float32)
    mask8 = np.zeros((P, P), np.float32)
    mask8[j // DH, j] = 1.0
    maskp = np.stack([(j // DH) % 2 == 0, (j // DH) % 2 == 1], axis=1).astype(np.float32)
    hot = np.zeros((P, H), np.float32)
    hot[KR + np.arange(H), np.arange(H)] = 1.0
    parts = {
        "wtok": np.concatenate([f(n)[:, perm] for n in ("L0_tok_Wf", "L0_tok_Wi", "L0_tok_Wh")], axis=1),
        "btok": np.stack([f(n)[perm] for n in ("L0_tok_bf", "L0_tok_bi", "L0_tok_bh")], axis=1),
        "cmat": eye - np.float32(1.0 / P), "omat": np.full((P, P), 1.0 / P, np.float32),
        "wq": f("L0_attn_q_w")[:, perm].T, "wk": f("L0_attn_kv_w")[:D, perm].T, "wv": f("L0_attn_kv_w")[D:, perm].T,
        "ident": eye, "ones32": np.concatenate([one16, zero16, zero16, one16], axis=1), "mask8": mask8,
        "maskp": maskp, "hot": hot, "gate_w": f("L0_ffn_gate_w")[perm], "gate_b": np.repeat(f("L0_ffn_gate_b")[None], P, axis=0),
        "rank": np.repeat(np.arange(E, 0, -1, dtype=np.float32)[None], P, axis=0), "b2": b2s,
        "par": np.concatenate(params, axis=1),
    }
    consts = np.concatenate([parts[n] for n in CONSTS], axis=1)
    sel = np.zeros((P, NF, P), np.float32)
    for n in range(NE * I):
        sel[n // I, n // P, n % P] = 1.0
        sel[32 + n // I, n // P, n % P] = 1.0
    arrays = {"x": x, "consts": consts, "sel": sel.reshape(P, -1), "w1": w1, "w2": w2}
    return {k: np.ascontiguousarray(a) for k, a in arrays.items()}


def kernel(**inputs):
    import concourse.bacc as bacc
    from concourse.bass_utils import run_bass_kernel_spmd

    nc = bacc.Bacc("TRN2", target_bir_lowering=False, num_devices=1)
    arrays = {f"in_{k}": a for k, a in layout(inputs).items()}
    args = [nc.dram_tensor(k, a.shape, mybir.dt.from_np(a.dtype), kind="ExternalInput").ap() for k, a in arrays.items()]
    out = nc.dram_tensor("out", (B, N, D), F32, kind="ExternalOutput").ap()
    spill = nc.dram_tensor("spill", (UNITS, 4, P, 2, W), F32, kind="Internal").ap()
    build(nc, *args, spill, out)
    r = run_bass_kernel_spmd(nc, [arrays], core_ids=[0])
    return r.results[0]["out"]
```

```python
from contextlib import ExitStack

import numpy as np
import concourse.bass as bass
from concourse import mybir

F32 = mybir.dt.float32
F32R = mybir.dt.float32r
ALU = mybir.AluOpType
ACT = mybir.ActivationFunctionType
AX_X = mybir.AxisListType.X

P = 128
B, T, D = 8, 256, 128
N = T + 1
W = N + 1
UNITS = B // 2
H, DH = 8, 16
PAIRS = H // 2
E, I = 16, 96
NE = E + 1
NF = -(-NE * I // P)
CH = 5
SCORE_SCALE = float(D) ** -0.5
EPS = 1e-5
SET_EXP_LN = 6
SET_EXP_TANH = 0
STEP = 3
LAST = slice(2 * W - 2 - STEP * (P - 1), 2 * W - 1, STEP)
ROWS = ((N - 1 - LAST.start) // STEP, P - 1)

CONSTS = {}
_at = 0
for _name, _n in (("wtok", 3 * P), ("btok", 3), ("cmat", P), ("omat", P), ("wq", P), ("wk", P), ("wv", P),
                  ("ident", P), ("ones32", 64), ("mask8", P), ("maskp", 2), ("hot", H), ("gate_w", E),
                  ("gate_b", E), ("rank", E), ("b2", P), ("par", 7 * NF)):
    CONSTS[_name] = (_at, _at + _n)
    _at += _n
NCONST = _at
NFIRST = CONSTS["wq"][0]
KR = 96
NSLOT = 4

NB = 3
NTE = 8
BURSTS = ((0, 4), (4, 8), (8, NF))
ROUTE = 5
BY_POOL = (0, 1, 4, 6, 7, 10)

TIMES = {
    "FAT": {
        "chunk": {"g": 0.0, "clip_up_1": 0.29, "u": 0.44, "gated_1": 0.69, "cw_1": 0.67, "clip_gate": 0.47},
        "down": (5.95, 10.4, 13.93),
        "add": (6.22, 10.25, 14.63),
        "out": 17.9,
        "attend": ({"begin": 0.0, "max": 0.2, "mlast": 0.25, "mtop": 0.35, "plast": 0.41, "st": 0.36, "pv": 0.2, "norm": 0.2},
                   {"begin": 1.65, "max": 0.4, "mlast": 0.31, "mtop": 0.3, "plast": 0.4, "st": 0.22, "pv": 0.2, "norm": 0.21}),
        "norm": {"center": 9.1, "variance": 10.05, "scale": 10.76, "gate": 12.11},
        "route": (12.16, 13.44, 13.84, 13.95, 14.05),
        "late": {"split": 14.98, "cwt": 15.0, "keep": 15.83},
        "token": (-0.27, 1.08, 1.46, 2.69, 3.78, 5.46, 6.46, 7.12, 7.66, 8.53),
        "project": {"center": 9.11, "variance": 10.11, "scale": 11.11, "project": 12.38},
    },
    "FA": {
        "chunk": {"g": 0.0, "clip_up_1": 0.0, "u": 0.52, "gated_1": 0.69, "cw_1": 0.7, "clip_gate": 0.47},
        "down": (6.1, 10.26, 13.93),
        "add": (6.22, 10.25, 14.9),
        "out": 17.27,
        "attend": ({"begin": 0.0, "max": 0.2, "mlast": 0.2, "mtop": 0.35, "plast": 0.35, "st": 0.36, "pv": 0.19, "norm": 0.2},
                   {"begin": 1.65, "max": 0.4, "mlast": 0.3, "mtop": 0.3, "plast": 0.4, "st": 0.22, "pv": 0.2, "norm": 0.2}),
        "norm": {"center": 9.1, "variance": 10.05, "scale": 11.38, "gate": 12.1},
        "route": (12.68, 13.66, 14.06, 14.17, 14.45),
        "late": {"split": 15.0, "cwt": 15.1, "keep": 16.01},
    },
    "F": {
        "chunk": {"g": 0.0, "clip_up_1": 0.11, "u": 0.4, "gated_1": 0.69, "cw_1": 0.7, "clip_gate": 0.47},
        "down": (5.69, 10.26, 13.85),
        "add": (6.22, 10.25, 14.63),
        "out": 17.19,
    },
    "AT": {
        "attend": ({"begin": -0.09, "max": 0.2, "mlast": 0.21, "mtop": 0.5, "plast": 0.33, "st": 0.36, "pv": 0.15, "norm": 0.2},
                   {"begin": 1.65, "max": 0.4, "mlast": 0.37, "mtop": 0.33, "plast": 0.4, "st": 0.22, "pv": 0.2, "norm": 0.43}),
        "norm": {"center": 9.1, "variance": 10.05, "scale": 11.1, "gate": 12.02},
        "route": (12.16, 13.23, 13.66, 14.06, 14.07),
        "late": {"split": 16.08, "cwt": 15.2, "keep": 15.29},
        "token": (-1.21, -1.19, -1.09, -1.0, -0.9, 0.41, 3.08, 4.57, 4.58, 8.65),
        "project": {"center": 9.26, "variance": 10.82, "scale": 11.79, "project": 12.67},
    },
    "T": {
        "token": (-1.21, -1.19, -1.09, -1.0, -0.9, 0.41, 3.08, 4.57, 4.58, 8.65),
        "project": {"center": 9.26, "variance": 10.82, "scale": 11.79, "project": 12.67},
    },
}


def attention_pieces(s):
    of_heads = lambda name: [(name, s, c, t) for c in range(2) for t in range(PAIRS)]
    return of_heads("max") + [("mlast", s), ("mtop", s), ("plast", s)] + of_heads("st") + [("pv", s), ("norm", s)]


def plan(f, a, t):
    times = TIMES["F" * f + "A" * a + "T" * t]
    at = []

    def place(stage, when, *piece):
        at.append((when, stage, *piece))

    if f:
        for c in range(NF + 1):
            for name, when in times["chunk"].items():
                before = name.endswith("_1")
                if 0 <= c - before < NF:
                    place("F", c + when, name.removesuffix("_1"), c - before)
        for piece in ("down", "add"):
            for burst, when in enumerate(times[piece]):
                place("F", when, piece, burst)
        place("F", times["out"], "out")
    if a:
        for batch, lengths in enumerate(times["attend"]):
            when = lengths["begin"]
            for name, *numbers in attention_pieces(batch):
                place("A", when, name, *numbers)
                when += lengths[name]
        for name, when in times["norm"].items():
            place("A", when, name, *((2,) if name != "gate" else ()))
        for k, when in enumerate(times["route"]):
            place("A", when, "route", k)
        for name, when in times["late"].items():
            place("A", when, name)
    if t:
        for k, when in enumerate(times["token"]):
            place("T", when, "token", k)
        for name, when in times["project"].items():
            place("T", when, name, *((1,) if name != "project" else ()))
    return [piece for _, *piece in sorted(at, key=lambda x: x[0])]


SLOTS_OF = {"g": ("g",), "u": ("u",), "cw": ("cw",), "max": ("max",), "mlast": ("mlast",), "plast": ("plast",),
            "st": ("st",), "pv": ("pv",), "center": ("cent",), "variance": ("var",), "scale": ("xc",),
            "project": ("q", "k", "v0", "v1"), "gate": ("gate",), "cwt": ("cwt",), "down": ("down",), "out": ("out",)}



def slot_uses(pieces):
    uses = []
    for _, piece, *numbers in pieces:
        names = ("zf", "zi", "zh") if (piece, numbers) == ("token", [0]) else SLOTS_OF.get(piece, ())
        uses += [(n, *numbers) if piece != "token" else (n,) for n in names]
    return uses


STEPS = {-2: (0, 0, 1), -1: (0, 1, 1), 0: (1, 1, 1), 2: (1, 1, 0), 3: (1, 0, 0)}
LOOPED = UNITS - 2
PLANS = {i: plan(*stages) for i, stages in STEPS.items()}
USES = {i: {name: n for n, name in enumerate(slot_uses(p))} for i, p in PLANS.items()}
assert len(USES[0]) % NSLOT == 0
BASE = {}
_at = 0
for _i in STEPS:
    BASE[_i] = _at
    _at += len(USES[_i]) * (LOOPED if _i == 0 else 1)


class Step:

    def __init__(self, kind, i):
        self.kind, self.i = kind, i
        self.plan = PLANS[kind]

    def unit(self, stage):
        return self.i + {"F": 0, "A": 1, "T": 2}[stage]

    def use(self, name):
        n = BASE[self.kind] + USES[self.kind][name]
        before = n // NSLOT
        if self.kind == 0:
            before = self.i * (len(USES[0]) // NSLOT) + before
        return n % NSLOT, before


def build(nc, x_in, consts_in, sel_in, w1_in, w2_in, spill, out):
    ctx = ExitStack()
    with ctx:
        def sb(name, shape, dt=F32):
            return ctx.enter_context(nc.sbuf_tensor(name, shape, dt))

        def sem(name):
            return ctx.enter_context(nc.semaphore(name))

        cst = sb("cst", [P, NCONST])
        sel = sb("sel", [P, NF, P], F32R)
        w1h = sb("w1h", [P, 2, NF, P], F32R)
        w1l = sb("w1l", [P, 2, NF, P], F32R)
        w2 = sb("w2", [P, NF, P])
        fpar = sb("fpar", [P, 7, NF])
        clt = sb("clt", [P, 3, 2 * NF])
        one = sb("one", [P, 1])
        eps = sb("eps", [P, 1])
        credit = sb("credit", [P, 1])
        xt = sb("xt", [P, 2, T])
        zs = sb("zs", [P, 3, 2, T])
        earg = zs
        fexp = sb("fexp", [P, 2, T])
        zmin = sb("zmin", [P, 3, 2, T])
        zpos = sb("zpos", [P, 2, T])
        zabs = sb("zabs", [P, 2, 2, T])
        xn1 = sb("xn1", [P, 2, W])
        stat1 = sb("stat1", [P, 2, W])
        dlog, wlog = xn1[:, :, 0:T], stat1[:, :, 0:T]
        drel = sb("drel", [P, 2, T])
        rmax = sb("rmax", [P, 2, N])
        half = sb("half", [P, 2, T])
        gate = sb("gate", [P, 2, T])
        state = sb("state", [P, 2, T])
        h1 = sb("h1", [P, 2, W])
        qhl = sb("qhl", [P, 2, 2, W], F32R)
        khl = sb("khl", [P, 2, 2, W], F32R)
        qh, ql, kh, kl = qhl[:, 0], qhl[:, 1], khl[:, 0], khl[:, 1]
        qs = sb("qs", [KR + H, 2, PAIRS, W], F32R)
        ks = sb("ks", [KR + H, 2, PAIRS, 2, W], F32R)
        vpad = sb("vpad", [P, 2, 2, H, 32])
        vlast = sb("vlast", [P, 2, P])
        bq = sb("bq", [KR, 2, 4 * P + 8], F32R)
        bk = sb("bk", [KR + H, 2, 4 * P + 8], F32R)
        mx = sb("mx", [P, 2, 2, H])
        mxl = sb("mxl", [P, 2])
        pt = sb("pt", [P, 2, H, W])
        pl = sb("pl", [P, 2, W])
        rden = sb("rden", [P, W])
        h2n = sb("h2n", [P, 2, W])
        xn2 = sb("xn2", [P, 2, W])
        stat2 = sb("stat2", [P, 2, W])
        gl = sb("gl", [P, 4, CH, E])
        oh = sb("oh", [P, 2, CH, E])
        gm = sb("gm", [P, 8, CH])
        cw = sb("cw", [P, CH, NE])
        cw2 = sb("cw2", [P, CH, E])
        cwp = sb("cwp", [P, CH, P])
        xh = sb("xh", [P, 2, W], F32R)
        xl = sb("xl", [P, 2, W], F32R)
        cwt = sb("cwt", [P, 2, W], F32R)
        h2 = sb("h2", [P, 2, W])
        gbuf = sb("gbuf", [P, NB, 2, W])
        ubuf = sb("ubuf", [P, NB, 2, W])
        tbuf = sb("tbuf", [P, NB, 2, W])
        cwb = sb("cwb", [P, 2, W])
        te = sb("te", [P, NTE, 2, W])
        yo = stat2
        osb = sb("osb", [P, CH, P])
        sel_stage = te[:, :, :, :].rearrange("p c s n -> p (c s n)")[:, 0:NF * P]
        w1_stage = pt[:, :, :, :].rearrange("p c h n -> p (c h n)")[:, 0:2 * NF * P]

        slot_mem = [ctx.enter_context(nc.psum_tensor(f"slot{i}", [P, 2, 512], F32)) for i in range(NSLOT)]

        def const(name):
            a, b = CONSTS[name]
            return cst[:, a:b]

        ident = const("ident")
        par = const("par").rearrange("p (k c) -> p k c", c=NF)
        B1G, B1U, ALPHA, GSCALE, SHIFT, CLG, CLU = range(7)
        UB, HA, GHI, GLO, UHI, ULO, WSC = range(7)

        full = [sem(f"psum_full{i}") for i in range(NSLOT)]
        free = [sem(f"psum_free{i}") for i in range(NSLOT)]
        s_first, s_const, s_sel = sem("first_loaded"), sem("const_loaded"), sem("sel_loaded")
        s_w1, s_w2 = sem("w1_loaded"), sem("w2_loaded")
        s_x, s_out = sem("x_loaded"), sem("out_stored")
        s_init, s_clear, s_hot = sem("constants_set"), sem("tiles_cleared"), sem("hot_rows_written")
        s_zero, s_high = sem("tiles_zeroed"), sem("high_weights")
        s_seta, s_setd = sem("act_setup"), sem("dve_setup")
        names = ("zmin zpos zabs ef ti tm ucw dlog wlog rmax half drel rfac gfac dec trm rar fin ed eq er "
                 "efin rg rr den term state rec es h1 rs1 rs2 qh kh vpad spill_q spill_k stack bq bk nm "
                 "nml rden h2n h2 xh xl cwl gtop gexp gclip uclip th gg te").split()
        S = {n: sem("r_" + n) for n in names}

        block = ctx.enter_context(nc.Block())

        def ge(eng, name, value):
            if not isinstance(value, int) or value > 0:
                eng.wait_ge(S[name] if isinstance(name, str) else name, value)

        def slot(st, name):
            return slot_mem[st.use(name)[0]]

        def take(eng, st, name):
            i, before = st.use(name)
            ge(eng, free[i], before)

        def filled(eng, st, name):
            i, before = st.use(name)
            eng.wait_ge(full[i], before + 1)

        def released(eng, st, name):
            i, before = st.use(name)
            eng.wait_ge(free[i], before + 1)

        def fill(instr, st, name):
            instr.then_inc(full[st.use(name)[0]], 1)

        def release(instr, st, name):
            instr.then_inc(free[st.use(name)[0]], 1)

        def run(eng, pieces, unrolled=False):
            def step(kind, i):
                st = Step(kind, i)
                for stage, piece, *numbers in st.plan:
                    if piece in pieces:
                        pieces[piece](st, st.unit(stage), *numbers)

            step(-2, -2)
            step(-1, -1)
            if unrolled:
                for i in range(LOOPED):
                    step(0, i)
            else:
                with eng.Fori(0, LOOPED) as i:
                    step(0, i)
            step(LOOPED, LOOPED)
            step(LOOPED + 1, LOOPED + 1)

        x_units = x_in.rearrange("p (u s t) -> u p s t", u=UNITS, s=2)
        out_units = out.rearrange("(s u) n c -> u s n c", s=2)
        NSTACK = 9
        SMALL = 19
        SETUP = 10
        INIT = 4
        ZEROED = 7

        @block.sync
        def _(sp):
            sp.dma_start(xt[:, :, :], x_units[0]).then_inc(s_x, 16)
            sp.dma_start(cst[:, 0:NFIRST], consts_in[:, 0:NFIRST]).then_inc(s_first, 16)
            sp.dma_start(cst[:, NFIRST:], consts_in[:, NFIRST:]).then_inc(s_const, 16)
            sp.dma_start(w1_stage, w1_in).then_inc(s_w1, 16)
            sp.dma_start(sel_stage, sel_in).then_inc(s_sel, 16)
            sp.dma_start(w2[:, :, :], w2_in.rearrange("p (c n) -> p c n", n=P)).then_inc(s_w2, 16)

            def token(st, u, k):
                if k == 1 and u + 1 < UNITS:
                    released(sp, st, ("zh",))
                    sp.dma_start(xt[:, :, :], x_units[u + 1]).then_inc(s_x, 16)

            def project(st, u):
                for k, name in enumerate(("q", "k")):
                    ge(sp, name + "h", u + 1)
                    released(sp, st, (name,))
                    sp.dma_start(spill[u][2 * k:2 * k + 2].rearrange("k p s n -> p k s n"),
                                 (qhl, khl)[k][:, :, :, :].bitcast(F32)).then_inc(S["spill_" + name], 16)
                if st.kind == -2:
                    sp.wait_ge(s_zero, 1)
                ge(sp, "h2n", 2 * u)
                sp.wait_ge(S["spill_q"], 16 * (u + 1))
                for r, src in enumerate((0, 1, 0)):
                    sp.dma_start(qs[32 * r:32 * r + 32, :, :, :].bitcast(F32),
                                 spill[u][src].rearrange("(t p) s n -> p s t n", p=32)).then_inc(S["stack"], 16)
                sp.wait_ge(S["spill_k"], 16 * (u + 1))
                for r, src in enumerate((2, 2, 3)):
                    by_head = spill[u][src].rearrange("(t i p) s n -> i p s t n", i=2, p=16)
                    for i in range(2):
                        sp.dma_start(ks[32 * r + 16 * i:32 * r + 16 * i + 16, :, :, i, :].bitcast(F32), by_head[i])\
                          .then_inc(S["stack"], 16)

            def store(st, u):
                released(sp, st, ("out",))
                for s in range(2):
                    dst = out_units[u]
                    sp.dma_start(dst[s, 0:256, :].rearrange("(c p) n -> p c n", p=P), osb[:, 2 * s:2 * s + 2, :])\
                      .then_inc(s_out, 16)
                    sp.dma_start(dst[s, 256:257, :], osb[ROWS[s]:ROWS[s] + 1, 4, :]).then_inc(s_out, 16)

            run(sp, {"token": token, "project": project, "out": store}, unrolled=True)
            sp.wait_ge(s_out, 64 * UNITS + 1)

        def mixer_products(e, eng, st, u, k):
            if k == 2:
                ge(eng, "zmin", u + 1)
                e.tensor_tensor(dlog, zmin[:, 1, :, :], zmin[:, 0, :, :], ALU.subtract).then_inc(S["dlog"], 1)
                ge(eng, "ef", u + 1)
                ge(eng, "dlog", u + 1)
                e.tensor_tensor(wlog, dlog, zmin[:, 2, :, :], ALU.add).then_inc(S["wlog"], 1)
                e.tensor_scalar(half[:, :, :], zabs[:, 0, :, :], 1.0, 0.5, ALU.add, ALU.mult).then_inc(S["half"], 1)
            elif k == 4:
                ge(eng, "rmax", 2 * u + 2)
                ge(eng, "es", u)
                e.tensor_tensor(earg[:, 0, :, :], rmax[:, :, 0:T], rmax[:, :, 1:N], ALU.subtract).then_inc(S["dec"], 1)
                e.tensor_tensor(earg[:, 1, :, :], wlog, rmax[:, :, 1:N], ALU.subtract).then_inc(S["trm"], 1)
                ge(eng, "drel", u + 1)
                e.tensor_tensor(earg[:, 2, :, :], dlog, drel[:, :, :], ALU.subtract).then_inc(S["rar"], 1)
                e.tensor_tensor(fexp[:, :, :], rmax[:, :, 1:N], drel[:, :, :], ALU.subtract).then_inc(S["fin"], 1)
            elif k == 6:
                ge(eng, "rfac", u + 1)
                ge(eng, "gfac", u + 1)
                e.tensor_tensor(gate[:, :, :], gate[:, :, :], half[:, :, :], ALU.mult).then_inc(S["rg"], 1)
                ge(eng, "er", u + 1)
                e.tensor_tensor(earg[:, 2, :, :], earg[:, 2, :, :], half[:, :, :], ALU.mult).then_inc(S["rr"], 1)
                ge(eng, "rr", u + 1)
                ge(eng, "eq", u + 1)
                e.tensor_tensor(earg[:, 2, :, :], earg[:, 2, :, :], drel[:, :, :], ALU.add).then_inc(S["den"], 1)
                ge(eng, "ed", u + 1)
                e.tensor_tensor(gate[:, :, :], gate[:, :, :], earg[:, 1, :, :], ALU.mult).then_inc(S["term"], 1)
            elif k == 8:
                ge(eng, "state", 2 * u + 2)
                ge(eng, "efin", u + 1)
                e.tensor_tensor(state[:, :, :], fexp[:, :, :], state[:, :, :], ALU.mult).then_inc(S["es"], 1)
            elif k == 9:
                ge(eng, "rec", 2 * u + 2)
                ge(eng, "es", u + 1)
                ge(eng, "h2n", 2 * u)
                e.tensor_tensor(h1[:, :, 1:N], earg[:, 2, :, :], state[:, :, :], ALU.mult).then_inc(S["h1"], 1)

        @block.gpsimd
        def _(pool):
            pool.memset(one[:, :], 1.0).then_inc(s_init, 1)
            pool.memset(eps[:, :], EPS).then_inc(s_init, 1)
            pool.memset(rmax[:, :, 0:1], 0.0).then_inc(s_init, 1)
            pool.memset(h1[:, :, :], 0.5).then_inc(s_init, 1)
            pool.wait_ge(s_init, 4)
            pool.memset(credit[:, :], 1.0).then_inc(s_out, 1)
            pool.wait_ge(s_out, 1)
            pool.memset(vpad[:, :, :, :, :], 0.0).then_inc(s_clear, 1)

            g = nc.gpsimd

            def token(st, u, k):
                if st.kind != -2:
                    mixer_products(g, pool, st, u, k)

            def cw_(st, u, c):
                if c in BY_POOL:
                    released(pool, st, ("cw", c))
                    ge(pool, "uclip", NF * u + c + 1)
                    g.tensor_tensor(ubuf[:, c % NB, :, :], ubuf[:, c % NB, :, :], cwb[:, :, :],
                                    ALU.mult).then_inc(S["ucw"], 1)
                ge(pool, "gg", NF * u + c + 1)
                if c in BY_POOL:
                    ge(pool, "ucw", len(BY_POOL) * u + BY_POOL.index(c) + 1)
                else:
                    released(pool, st, ("cw", c))
                if c >= NTE:
                    burst = next(b for b, (_, end) in enumerate(BURSTS) if end > c - NTE)
                    filled(pool, st, ("down", burst))
                g.tensor_tensor(te[:, c % NTE, :, :], tbuf[:, c % NB, :, :], ubuf[:, c % NB, :, :], ALU.mult)\
                    .then_inc(S["te"], 1)

            pool.wait_ge(s_clear, 1)
            run(pool, {"token": token, "cw": cw_})

        @block.scalar
        def _(act):
            a = nc.scalar.activation

            def tables(number):
                nc.scalar.add_instruction(mybir.InstLoadActFuncSet(
                    name=nc.get_next_instruction_name(), act_func_set_id=number, ins=[], outs=[]))

            def token(st, u, k):
                flat = lambda ap: ap.rearrange("p s t -> p (s t)")
                btok = const("btok")
                if k == 0:
                    ge(act, "h1", u)
                    for j, name in enumerate(("zf", "zi", "zh")):
                        filled(act, st, (name,))
                        z = slot(st, (name,))[:, 0, :]
                        release(a(flat(zs[:, j, :, :]), z, ACT.Identity, bias=btok[:, j:j + 1]), st, (name,))
                elif k == 1:
                    released(act, st, ("zi",))
                    a(zabs[:, :, :, :], zs[:, 0:2, :, :], ACT.Abs).then_inc(S["zabs"], 1)
                elif k == 2:
                    ge(act, "zabs", u + 1)
                    a(zabs[:, 0, :, :], zabs[:, 0, :, :], ACT.Exp, scale=-1.0).then_inc(S["ef"], 1)
                    a(zabs[:, 1, :, :], zabs[:, 1, :, :], ACT.Tanh, scale=0.5).then_inc(S["ti"], 1)
                    ge(act, "zmin", u + 1)
                    a(gate[:, :, :], zmin[:, 2, :, :], ACT.Tanh, scale=0.5).then_inc(S["tm"], 1)
                elif k == 3:
                    ge(act, "dlog", u + 1)
                    a(drel[:, :, :], dlog, ACT.Relu).then_inc(S["drel"], 1)
                elif k == 5:
                    ge(act, "dec", u + 1)
                    ge(act, "trm", u + 1)
                    a(earg[:, 0:2, :, :], earg[:, 0:2, :, :], ACT.Exp).then_inc(S["ed"], 1)
                    ge(act, "rar", u + 1)
                    a(earg[:, 2, :, :], earg[:, 2, :, :], ACT.Exp).then_inc(S["er"], 1)
                    ge(act, "fin", u + 1)
                    a(drel[:, :, :], drel[:, :, :], ACT.Exp, scale=-1.0).then_inc(S["eq"], 1)
                    a(fexp[:, :, :], fexp[:, :, :], ACT.Exp).then_inc(S["efin"], 1)
                    if st.kind == -2:
                        tables(SET_EXP_LN)
                        act.wait_ge(s_w1, 16)
                        a(w1h[:, :, :, :].rearrange("p k c n -> p (k c n)"), w1_stage, ACT.Copy).then_inc(s_high, 1)
                        act.wait_ge(s_sel, 16)
                        a(sel[:, :, :].rearrange("p c n -> p (c n)"), sel_stage, ACT.Copy).then_inc(s_high, 1)

            def center(st, u, which):
                stat = (stat1, stat2)[which - 1]
                if which == 2 and st.kind == -1:
                    tables(SET_EXP_LN)
                filled(act, st, ("cent", which))
                release(a(stat[:, :, :], slot(st, ("cent", which))[:, :, 0:W], ACT.Square), st, ("cent", which))

            def variance(st, u, which):
                stat = (stat1, stat2)[which - 1]
                if which == 2 and st.kind != -1:
                    tables(SET_EXP_LN)
                filled(act, st, ("var", which))
                var = slot(st, ("var", which))[:, :, 0:W]
                release(a(stat[:, :, :], var, ACT.Ln, bias=eps[:, :]), st, ("var", which))
                released(act, st, ("var", which))
                a(stat[:, :, :], stat[:, :, :], ACT.Exp, scale=-0.5).then_inc(S[f"rs{which}"], 1)
                if st.kind == -2:
                    clamps()
                if which == 1 or st.kind == LOOPED:
                    tables(SET_EXP_TANH)

            def project(st, u):
                filled(act, st, ("q",))
                a(qh[:, :, :], slot(st, ("q",))[:, :, 0:W], ACT.Copy).then_inc(S["qh"], 1)
                filled(act, st, ("k",))
                a(kh[:, :, :], slot(st, ("k",))[:, :, 0:W], ACT.Copy).then_inc(S["kh"], 1)
                if st.kind == -2:
                    act.wait_ge(s_clear, 1)
                ge(act, "h2n", 2 * u)
                for s in range(2):
                    dst = vpad[:, s, :, :, :].rearrange("p c (j i) x -> p (c j) (i x)", i=2)
                    filled(act, st, (f"v{s}",))
                    src = slot(st, (f"v{s}",))[:, 0, 0:256].rearrange("p (cj i x) -> p cj i x", i=2, x=DH)
                    for i in range(2):
                        a(dst[:, :, 48 * i:48 * i + DH], src[:, :, i, :], ACT.Copy).then_inc(S["vpad"], 1)

            def mlast(st, u, s):
                name = ("mlast", s)
                filled(act, st, name)
                a(qs[KR:KR + H, s, :, 0:256], slot(st, name)[KR:KR + H, 1:2, 0:256].to_broadcast([H, PAIRS, 256]),
                  ACT.Copy, scale=-1.0).then_inc(S["nm"], 1)

            def plast(st, u, s):
                name = ("plast", s)
                filled(act, st, name)
                release(a(pl[:, s, :], slot(st, name)[:, 0, 0:W], ACT.Exp, scale=SCORE_SCALE), st, name)

            def st_(st, u, s, c, t):
                name = ("st", s, c, t)
                if (c, t) == (0, 0):
                    if s:
                        filled(act, st, ("pv", 0))
                    elif st.kind == -1:
                        act.wait_ge(s_setd, SETUP)
                    else:
                        ge(act, "h2n", 2 * u)
                filled(act, st, name)
                scores = slot(st, name)[:, :, 0:W]
                release(a(pt[:, c, 2 * t:2 * t + 2, :], scores, ACT.Exp, scale=SCORE_SCALE), st, name)

            def split(st, u):
                released(act, st, ("xc", 2))
                if st.kind != -1:
                    filled(act, st, ("u", NF - 1))
                a(xh[:, :, :], xn2[:, :, :], ACT.Copy).then_inc(S["xh"], 1)

            def route(st, u, k):
                if k == ROUTE - 2:
                    ge(act, "gtop", u + 1)
                    a(gm[:, 5, :], gm[:, 4, :], ACT.Exp).then_inc(S["gexp"], 1)

            def cwt_(st, u):
                filled(act, st, ("cwt",))
                a(cwt[:, :, 0:256], slot(st, ("cwt",))[:, 0, :].rearrange("p (s t) -> p s t", s=2), ACT.Copy)
                release(a(cwt[:, :, 256], slot(st, ("cwt",))[:, 1, ROWS[0]:ROWS[1] + 1:ROWS[1] - ROWS[0]], ACT.Copy),
                        st, ("cwt",))

            def keep(st, u):
                if st.kind != -1:
                    released(act, st, ("down", len(BURSTS) - 1))
                a(h2[:, :, :], h2n[:, :, :], ACT.Copy).then_inc(S["h2"], 1)

            def gate_half(st, u, c):
                filled(act, st, ("g", c))
                if c >= NB:
                    ge(act, "gg", NF * u + c + 1 - NB)
                release(a(gbuf[:, c % NB, :, :], slot(st, ("g", c))[:, :, 0:W], ACT.Identity, bias=par[:, B1G, c:c + 1]),
                        st, ("g", c))
                if c:
                    tanh(u, c - 1)

            def up_half(st, u, c):
                filled(act, st, ("u", c))
                if c >= NB:
                    ge(act, "te", NF * u + c + 1 - NB)
                release(a(ubuf[:, c % NB, :, :], slot(st, ("u", c))[:, :, 0:W], ACT.Identity, bias=fpar[:, UB, c:c + 1]),
                        st, ("u", c))
                if c == NF - 1:
                    tanh(u, c)

            def cw_(st, u, c):
                if c in BY_POOL:
                    n = BY_POOL.index(c)
                    filled(act, st, ("cw", c))
                    if n:
                        ge(act, "ucw", len(BY_POOL) * u + n)
                    release(a(cwb[:, :, :], slot(st, ("cw", c))[:, :, 0:W], ACT.Copy), st, ("cw", c))

            def tanh(u, c):
                ge(act, "gclip", NF * u + c + 1)
                if c >= NB:
                    ge(act, "te", NF * u + c + 1 - NB)
                a(tbuf[:, c % NB, :, :], gbuf[:, c % NB, :, :], ACT.Tanh, scale=fpar[:, HA, c:c + 1])\
                    .then_inc(S["th"], 1)

            def out_(st, u):
                filled(act, st, ("out",))
                ge(act, s_out, 64 * u + 1)
                for k in range(CH):
                    last = a(osb[:, k, :].rearrange("p (d h) -> p h d", h=H),
                             slot(st, ("out",))[:, k // 4, (k % 4) * P:(k % 4 + 1) * P].rearrange("p (h d) -> p h d", h=H),
                             ACT.Copy)
                release(last, st, ("out",))

            def clamps():
                raw = par[:, CLG:CLU + 1, :].rearrange("p k c -> p (k c)")
                act.wait_ge(s_const, 16)
                a(clt[:, 0, :], raw, ACT.Abs).then_inc(s_seta, 1)
                act.wait_ge(s_seta, 1)
                a(clt[:, 1, :], clt[:, 0, :], ACT.Exp, scale=-1.0).then_inc(s_seta, 1)
                act.wait_ge(s_seta, 2)
                a(clt[:, 2, :], clt[:, 1, :], ACT.Ln, bias=one[:, :]).then_inc(s_seta, 1)

            tables(SET_EXP_TANH)
            act.wait_ge(s_init, INIT)
            act.wait_ge(s_first, 16)
            run(act, {"token": token, "center": center, "variance": variance, "project": project, "mlast": mlast,
                      "plast": plast, "st": st_, "split": split, "route": route, "cwt": cwt_, "keep": keep,
                      "g": gate_half, "u": up_half, "cw": cw_, "out": out_})

        @block.vector
        def _(dve):
            v = nc.vector

            def mixer(st, u, k):
                if k == 1:
                    released(dve, st, ("zh",))
                    ge(dve, "wlog", u)
                    v.tensor_scalar(zmin[:, :, :, :], zs[:, :, :, :], 0.0, None, ALU.min).then_inc(S["zmin"], 1)
                    v.tensor_scalar(zpos[:, :, :], zs[:, 2, :, :], 0.0, 0.5, ALU.max, ALU.add).then_inc(S["zpos"], 1)
                elif k == 3:
                    ge(dve, "wlog", u + 1)
                    for s in range(2):
                        v.tensor_tensor_scan(rmax[:, s, 1:N], wlog[:, s, :], wlog[:, s, :], 0.0, ALU.max, ALU.max)\
                            .then_inc(S["rmax"], 1)
                elif k == 4:
                    ge(dve, "tm", u + 1)
                    ge(dve, "zpos", u + 1)
                    v.scalar_tensor_tensor(gate[:, :, :], gate[:, :, :], -0.5, zpos[:, :, :], ALU.mult, ALU.add)\
                        .then_inc(S["gfac"], 1)
                    ge(dve, "ti", u + 1)
                    ge(dve, "half", u + 1)
                    v.scalar_tensor_tensor(half[:, :, :], zabs[:, 1, :, :], 1.0, half[:, :, :], ALU.add, ALU.mult)\
                        .then_inc(S["rfac"], 1)
                elif k == 7:
                    ge(dve, "den", u + 1)
                    v.reciprocal(earg[:, 2, 0, :], earg[:, 2, 0, :]).then_inc(S["rec"], 1)
                    ge(dve, "term", u + 1)
                    for s in range(2):
                        v.tensor_tensor_scan(state[:, s, :], earg[:, 0, s, :], gate[:, s, :], 0.5, ALU.mult, ALU.add)\
                            .then_inc(S["state"], 1)
                elif k == 8:
                    v.reciprocal(earg[:, 2, 1, :], earg[:, 2, 1, :]).then_inc(S["rec"], 1)

            def token(st, u, k):
                if st.kind == -2 and k == 4:
                    mixer_products(v, dve, st, u, k)
                mixer(st, u, k)
                if st.kind == -2 and k != 4:
                    mixer_products(v, dve, st, u, k)
                if st.kind == -2 and k == 9:
                    low_weights()

            def scale(st, u, which):
                name = ("xc", which)
                ge(dve, f"rs{which}", u + 1)
                filled(dve, st, name)
                xn, stat = ((xn1, stat1), (xn2, stat2))[which - 1]
                release(v.tensor_tensor(xn[:, :, :], slot(st, name)[:, :, 0:W], stat[:, :, :], ALU.mult), st, name)

            def project(st, u):
                for name, hi, lo in (("q", qh, ql), ("k", kh, kl)):
                    filled(dve, st, (name,))
                    ge(dve, name + "h", u + 1)
                    release(v.tensor_tensor(lo[:, :, :], slot(st, (name,))[:, :, 0:W], hi[:, :, :].bitcast(F32),
                                            ALU.subtract), st, (name,))
                for s in range(2):
                    name = (f"v{s}",)
                    filled(dve, st, name)
                    ge(dve, "vpad", 4 * u + 2 * s + 2)
                    release(v.tensor_tensor(vlast[:, s, :], slot(st, name)[:, 0, 256:384], const("mask8"), ALU.mult),
                            st, name)
                if st.kind == -2:
                    parameters()

            def last_position(u):
                ge(dve, "stack", 16 * NSTACK * (u + 1))
                for s in range(2):
                    dq = bq[:, s, :].rearrange("p (t x) -> p t x", x=130)[:, :, KR:KR + 2]
                    v.tensor_tensor(dq, qs[0:KR, s, :, 256:257].bitcast(F32).to_broadcast([KR, PAIRS, 2]),
                                    const("maskp")[0:KR, :].unsqueeze(1).to_broadcast([KR, PAIRS, 2]), ALU.mult)\
                        .then_inc(S["bq"], 1)
                    dk = bk[:, s, :].rearrange("p (t x) -> p t x", x=130)[:, :, 0:2]
                    v.tensor_copy(dk, ks[:, s, :, :, 256].bitcast(F32)).then_inc(S["bk"], 1)

            def max_(st, u, s, c, t):
                if (s, c, t) == (0, 0, 0):
                    last_position(u)
                name = ("max", s, c, t)
                filled(dve, st, name)
                release(v.tensor_reduce(mx[:, s, c, 2 * t:2 * t + 2], slot(st, name)[:, :, 0:N], AX_X, ALU.max), st, name)

            def mtop(st, u, s):
                name = ("mlast", s)
                filled(dve, st, name)
                ge(dve, "nm", 2 * u + s + 1)
                release(v.tensor_reduce(mxl[KR:KR + H, s:s + 1], slot(st, name)[KR:KR + H, 0, 0:N], AX_X, ALU.max), st, name)
                released(dve, st, name)
                v.tensor_scalar(qs[KR:KR + H, s, :, 256], mxl[KR:KR + H, s:s + 1].to_broadcast([H, PAIRS]), -1.0, None,
                                ALU.mult).then_inc(S["nml"], 1)

            def norm(st, u, s):
                name = ("pv", s)
                filled(dve, st, name)
                ge(dve, "h2n", 2 * u + s)
                v.reciprocal(rden[:, :], slot(st, name)[:, 1, 0:W]).then_inc(S["rden"], 1)
                ge(dve, "rden", 2 * u + s + 1)
                release(v.tensor_tensor(rden[:, :], slot(st, name)[:, 0, 0:W], rden[:, :], ALU.mult), st, name)
                released(dve, st, name)
                v.tensor_tensor(h2n[:, s, 0:N], rden[:, 0:N], h1[:, s, 0:N], ALU.add).then_inc(S["h2n"], 1)

            def wide(ap):
                return ap.unsqueeze(2).to_broadcast([P, CH, E])

            def gate_(st, u):
                filled(dve, st, ("gate",))
                release(v.tensor_tensor(gl[:, 0, :, :],
                                        slot(st, ("gate",))[:, 0, 0:CH * E].rearrange("p (k e) -> p k e", e=E),
                                        const("gate_b").unsqueeze(1).to_broadcast([P, CH, E]), ALU.add), st, ("gate",))

            def route(st, u, k):
                after = lambda n: ge(dve, "cwl", u * SMALL + n)
                done = lambda ins: ins.then_inc(S["cwl"], 1)
                rank = const("rank").unsqueeze(1).to_broadcast([P, CH, E])
                if k in (0, 1, 2):
                    r, n = ((0, 0), (0, 3), (1, 6))[k]
                    if k == 0:
                        released(dve, st, ("gate",))
                    else:
                        after(n)
                if k in (0, 2):
                    done(v.tensor_reduce(gm[:, r, :], gl[:, r, :, :], AX_X, ALU.max))
                    after(n + 1)
                    done(v.tensor_tensor(gl[:, 2, :, :], gl[:, r, :, :], wide(gm[:, r, :]), ALU.is_equal))
                    after(n + 2)
                    done(v.tensor_tensor(gl[:, 3, :, :], gl[:, 2, :, :], rank, ALU.mult))
                elif k == 1:
                    done(v.tensor_reduce(gm[:, 2, :], gl[:, 3, :, :], AX_X, ALU.max))
                    after(4)
                    done(v.tensor_tensor(oh[:, 0, :, :], rank, wide(gm[:, 2, :]), ALU.is_equal))
                    after(5)
                    done(v.scalar_tensor_tensor(gl[:, 1, :, :], oh[:, 0, :, :], -1e30, gl[:, 0, :, :], ALU.mult, ALU.add))
                elif k == 3:
                    v.tensor_tensor(gm[:, 4, :], gm[:, 1, :], gm[:, 0, :], ALU.subtract).then_inc(S["gtop"], 1)
                    after(9)
                    done(v.tensor_reduce(gm[:, 3, :], gl[:, 3, :, :], AX_X, ALU.max))
                    after(10)
                    done(v.tensor_tensor(oh[:, 1, :, :], rank, wide(gm[:, 3, :]), ALU.is_equal))
                elif k == 4:
                    ge(dve, "gexp", u + 1)
                    done(v.tensor_scalar(gm[:, 6, :], gm[:, 5, :], 1.0, None, ALU.add))
                    after(12)
                    done(v.reciprocal(gm[:, 7, :], gm[:, 6, :]))
                    after(13)
                    done(v.tensor_tensor(gm[:, 6, :], gm[:, 5, :], gm[:, 7, :], ALU.mult))
                    done(v.tensor_tensor(cw[:, :, 0:E], oh[:, 0, :, :], wide(gm[:, 7, :]), ALU.mult))
                    after(14)
                    done(v.tensor_tensor(cw2[:, :, :], oh[:, 1, :, :], wide(gm[:, 6, :]), ALU.mult))
                    after(16)
                    done(v.tensor_tensor(cw[:, :, 0:E], cw[:, :, 0:E], cw2[:, :, :], ALU.add))
                    after(17)
                    done(v.tensor_copy(cwp[:, :, 0:NE].bitcast(F32R), cw[:, :, :]))
                    after(18)
                    done(v.tensor_tensor(cwp[:, :, 32:32 + NE], cw[:, :, :], cwp[:, :, 0:NE], ALU.subtract))

            def split(st, u):
                ge(dve, "xh", u + 1)
                v.tensor_tensor(xl[:, :, :], xn2[:, :, :], xh[:, :, :].bitcast(F32), ALU.subtract).then_inc(S["xl"], 1)

            def clip_gate(st, u, c):
                released(dve, st, ("g", c))
                p = c % NB
                v.tensor_scalar(gbuf[:, p, :, :], gbuf[:, p, :, :], fpar[:, GHI, c:c + 1], fpar[:, GLO, c:c + 1],
                                ALU.min, ALU.max).then_inc(S["gclip"], 1)

            def clip_up(st, u, c):
                released(dve, st, ("u", c))
                p = c % NB
                v.tensor_scalar(ubuf[:, p, :, :], ubuf[:, p, :, :], fpar[:, UHI, c:c + 1], fpar[:, ULO, c:c + 1],
                                ALU.min, ALU.max).then_inc(S["uclip"], 1)

            def gated(st, u, c):
                p = c % NB
                ge(dve, "th", NF * u + c + 1)
                v.scalar_tensor_tensor(tbuf[:, p, :, :], tbuf[:, p, :, :], 1.0, gbuf[:, p, :, :], ALU.add, ALU.mult)\
                    .then_inc(S["gg"], 1)

            def cw_(st, u, c):
                if c in BY_POOL:
                    return
                p = c % NB
                filled(dve, st, ("cw", c))
                ge(dve, "uclip", NF * u + c + 1)
                release(v.tensor_tensor(ubuf[:, p, :, :], slot(st, ("cw", c))[:, :, 0:W], ubuf[:, p, :, :], ALU.mult),
                        st, ("cw", c))

            def add(st, u, b):
                name = ("down", b)
                filled(dve, st, name)
                if b == 0:
                    ge(dve, "h2", u + 1)
                else:
                    released(dve, st, ("down", b - 1))
                last = b == len(BURSTS) - 1
                release(v.tensor_tensor((yo if last else h2)[:, :, :], slot(st, name)[:, :, 0:W], h2[:, :, :], ALU.add),
                        st, name)

            steps = [0]

            def then(ins):
                steps[0] += 1
                ins.then_inc(s_setd, 1)
                dve.wait_ge(s_setd, steps[0])

            def parameters():
                raw = par[:, CLG:CLU + 1, :].rearrange("p k c -> p (k c)")
                dve.wait_ge(s_seta, 3)
                then(v.scalar_tensor_tensor(clt[:, 0, :], raw, 0.0, clt[:, 2, :], ALU.max, ALU.add))
                cg, cu = clt[:, 0, 0:NF], clt[:, 0, NF:2 * NF]
                then(v.tensor_copy(fpar[:, GHI, :], cg))
                then(v.tensor_scalar(fpar[:, GLO, :], cg, -1.0, None, ALU.mult))
                then(v.tensor_tensor(fpar[:, UHI, :], par[:, SHIFT, :], cu, ALU.add))
                then(v.tensor_tensor(fpar[:, ULO, :], par[:, SHIFT, :], cu, ALU.subtract))
                then(v.tensor_tensor(fpar[:, UB, :], par[:, B1U, :], par[:, SHIFT, :], ALU.add))
                then(v.tensor_scalar(fpar[:, HA, :], par[:, ALPHA, :], 0.5, None, ALU.mult))
                then(v.tensor_scalar(fpar[:, WSC, :], par[:, GSCALE, :], 0.5, None, ALU.mult))
                dve.wait_ge(s_w2, 16)
                then(v.tensor_tensor(w2[:, :, :], w2[:, :, :], fpar[:, WSC, :].unsqueeze(2).to_broadcast([P, NF, P]),
                                     ALU.mult))

            def low_weights():
                dve.wait_ge(s_high, 1)
                then(v.tensor_tensor(w1l[:, :, :, :].rearrange("p k c n -> p (k c n)"), w1_stage,
                                     w1h[:, :, :, :].rearrange("p k c n -> p (k c n)").bitcast(F32), ALU.subtract))

            for tile in (ks[0:KR, :, :, :, :], qs[KR:KR + H, :, :, N:W], bq[:, :, :], bk[:, :, :], cwt[:, :, N:W]):
                v.memset(tile.bitcast(F32), 0.0).then_inc(s_zero, 1)
            v.memset(h2n[:, :, N:W], 0.5).then_inc(s_zero, 1)
            v.memset(cwp[:, :, :], 0.0).then_inc(s_zero, 1)
            v.memset(cw[:, :, E:NE], 1.0)
            dve.wait_ge(s_const, 16)
            v.tensor_copy(ks[KR:KR + H, :, :, :, :].rearrange("p s t i n -> p s (t i) n"),
                          const("hot")[KR:KR + H, :].unsqueeze(1).unsqueeze(3).to_broadcast([H, 2, H, W])).then_inc(s_hot, 1)
            dve.wait_ge(s_first, 16)
            dve.wait_ge(s_init, INIT)
            run(dve, {"token": token, "scale": scale, "project": project, "max": max_, "mtop": mtop, "norm": norm,
                      "gate": gate_, "route": route, "split": split, "clip_gate": clip_gate, "clip_up": clip_up,
                      "gated": gated, "cw": cw_, "add": add})

        @block.tensor
        def _(pe):
            def mm(out_, lhsT, rhs, start=True, stop=True, **k):
                return nc.tensor.matmul(out_, lhsT, rhs, start=start, stop=stop, **k)

            def token(st, u, k):
                if k:
                    return
                pe.wait_ge(s_x, 16 * (u + 1))
                wtok = const("wtok").rearrange("p (k n) -> p k n", n=P)
                xall = xt[:, :, :].rearrange("p s t -> p (s t)")
                for j, name in enumerate(("zf", "zi", "zh")):
                    take(pe, st, (name,))
                    fill(mm(slot(st, (name,))[:, 0, :], wtok[:, j, :], xall), st, (name,))

            def centered(st, u, name, which):
                take(pe, st, name)
                ge(pe, ("h1", "h2n")[which - 1], (u + 1, 2 * u + 2)[which - 1])
                for s in range(2):
                    last = mm(slot(st, name)[:, s, 0:W], const("cmat"), (h1, h2n)[which - 1][:, s, :])
                fill(last, st, name)

            def center(st, u, which):
                centered(st, u, ("cent", which), which)

            def scale(st, u, which):
                centered(st, u, ("xc", which), which)

            def variance(st, u, which):
                name = ("var", which)
                take(pe, st, name)
                released(pe, st, ("cent", which))
                for s in range(2):
                    last = mm(slot(st, name)[:, s, 0:W], const("omat"), (stat1, stat2)[which - 1][:, s, :])
                fill(last, st, name)

            def project(st, u):
                if st.kind == -2:
                    pe.wait_ge(s_const, 16)
                released(pe, st, ("xc", 1))
                for name in ("q", "k"):
                    take(pe, st, (name,))
                    for s in range(2):
                        last = mm(slot(st, (name,))[:, s, 0:W], const("w" + name), xn1[:, s, :])
                    fill(last, st, (name,))
                for s in range(2):
                    name = (f"v{s}",)
                    take(pe, st, name)
                    for c in range(2):
                        mm(slot(st, name)[:, 0, c * P:(c + 1) * P], xn1[:, s, c * P:(c + 1) * P], const("wv"))
                    fill(mm(slot(st, name)[:, 0, 256:384], xn1[:, s, 256:257].to_broadcast([P, P]), const("wv")), st, name)

            def max_(st, u, s, c, t):
                name = ("max", s, c, t)
                if (s, c, t) == (0, 0, 0):
                    ge(pe, "stack", 16 * NSTACK * (u + 1))
                    if st.kind == -1:
                        pe.wait_ge(s_zero, ZEROED)
                        pe.wait_ge(s_hot, 1)
                take(pe, st, name)
                for i in range(2):
                    last = mm(slot(st, name)[:, i, 0:W], qs[0:KR, s, t, c * P:(c + 1) * P], ks[0:KR, 1 - s, t, i, :])
                fill(last, st, name)

            def mlast(st, u, s):
                name = ("mlast", s)
                take(pe, st, name)
                ge(pe, "bq", 2 * u + 2)
                for k in range(H):
                    t, i = divmod(k, 2)
                    mm(slot(st, name)[:, 0, 0:W], bq[:, s, t * P:(t + 1) * P], ks[0:KR, 1 - s, t, i, :],
                       start=(k == 0), stop=(k == H - 1))
                released(pe, st, ("max", s, 1, PAIRS - 1))
                for c in range(2):
                    last = mm(slot(st, name)[KR:KR + H, 1, c * P:(c + 1) * P], mx[:, s, c, :], ident)
                fill(last, st, name)

            def plast(st, u, s):
                name = ("plast", s)
                take(pe, st, name)
                ge(pe, "nm", 2 * u + s + 1)
                ge(pe, "nml", 2 * u + s + 1)
                ge(pe, "bk", 2 * u + 2)
                for t in range(PAIRS):
                    last = mm(slot(st, name)[:, 0, 0:W], bk[:, 1 - s, t * P:(t + 1) * P], qs[:, s, t, :],
                              start=(t == 0), stop=(t == PAIRS - 1))
                fill(last, st, name)

            def st_(st, u, s, c, t):
                name = ("st", s, c, t)
                take(pe, st, name)
                for i in range(2):
                    last = mm(slot(st, name)[:, i, 0:W], ks[:, 1 - s, t, i, c * P:(c + 1) * P], qs[:, s, t, :])
                fill(last, st, name)

            def pv(st, u, s):
                name = ("pv", s)
                take(pe, st, name)
                released(pe, st, ("plast", s))
                ge(pe, "vpad", 4 * u + 4)
                o = slot(st, name)
                mm(o[:, 0, 0:W], vlast[:, 1 - s, :], pl[:, s, :], stop=False)
                mm(o[:, 1, 0:W], const("mask8"), pl[:, s, :], stop=False)
                ones32 = const("ones32")
                for c in range(2):
                    released(pe, st, ("st", s, c, PAIRS - 1))
                    for i in range(2):
                        for bank in range(2):
                            for t in range(PAIRS):
                                lhsT = ones32[:, 32 * i:32 * i + 32] if bank else vpad[:, 1 - s, c, 2 * t + i, :]
                                last = mm(o[32 * t:32 * t + 32, bank, 0:W], lhsT, pt[:, c, 2 * t + i, :],
                                          start=False, stop=(c == 1 and i == 1))
                fill(last, st, name)

            def gate_(st, u):
                name = ("gate",)
                released(pe, st, ("xc", 2))
                take(pe, st, name)
                for k in range(CH):
                    s, c = divmod(k, 2)
                    lhsT = (xn2[:, s, c * P:(c + 1) * P] if k < 4
                            else xn2[:, :, :].rearrange("p s t -> p (s t)")[:, LAST])
                    last = mm(slot(st, name)[:, 0, k * E:(k + 1) * E], lhsT, const("gate_w"))
                fill(last, st, name)

            def cwt_(st, u):
                name = ("cwt",)
                take(pe, st, name)
                ge(pe, "cwl", SMALL * (u + 1))
                for k in range(CH):
                    last = nc.tensor.transpose(slot(st, name)[:, k // 4, (k % 4) * P:(k % 4 + 1) * P], cwp[:, k, :], ident)
                fill(last, st, name)

            def half_(st, u, c, k):
                name = ("gu"[k], c)
                if (c, k) == (0, 0):
                    ge(pe, "xl", u + 1)
                    if st.kind == 0:
                        pe.wait_ge(s_setd, SETUP)
                take(pe, st, name)
                for s in range(2):
                    o = slot(st, name)[:, s, 0:W]
                    mm(o, w1h[:, k, c, :], xh[:, s, :], stop=False)
                    mm(o, w1h[:, k, c, :], xl[:, s, :], start=False, stop=False)
                    last = mm(o, w1l[:, k, c, :], xh[:, s, :], start=False)
                fill(last, st, name)

            def gate_half(st, u, c):
                half_(st, u, c, 0)

            def up_half(st, u, c):
                half_(st, u, c, 1)

            def cw_(st, u, c):
                name = ("cw", c)
                take(pe, st, name)
                if c == 0:
                    pe.wait_ge(s_high, 2)
                    ge(pe, "h2", u + 1)
                for s in range(2):
                    last = mm(slot(st, name)[:, s, 0:W], sel[:, c, :], cwt[:, s, :])
                fill(last, st, name)

            def down(st, u, b):
                name = ("down", b)
                take(pe, st, name)
                begin, end = BURSTS[b]
                if b == 0:
                    for s in range(2):
                        mm(slot(st, name)[:, s, 0:W], const("b2"), cwt[:, s, :].bitcast(F32), stop=False)
                for c in range(begin, end):
                    ge(pe, "te", NF * u + c + 1)
                    for s in range(2):
                        last = mm(slot(st, name)[:, s, 0:W], w2[:, c, :], te[:, c % NTE, s, :],
                                  start=(c == begin and b > 0), stop=(c == end - 1))
                fill(last, st, name)

            def out_(st, u):
                name = ("out",)
                take(pe, st, name)
                released(pe, st, ("down", len(BURSTS) - 1))
                for k in range(CH):
                    s, c = divmod(k, 2)
                    src = yo[:, s, c * P:(c + 1) * P] if k < 4 else yo[:, :, :].rearrange("p s t -> p (s t)")[:, LAST]
                    last = nc.tensor.transpose(slot(st, name)[:, k // 4, (k % 4) * P:(k % 4 + 1) * P], src, ident)
                fill(last, st, name)

            pe.wait_ge(s_first, 16)
            pe.wait_ge(s_init, INIT)
            run(pe, {"token": token, "center": center, "variance": variance, "scale": scale, "project": project, "max": max_,
                     "mlast": mlast, "plast": plast, "st": st_, "pv": pv, "gate": gate_, "cwt": cwt_, "g": gate_half,
                     "u": up_half, "cw": cw_, "down": down, "out": out_})


def layout(inputs):
    f = lambda n: np.asarray(inputs[n])
    j = np.arange(P)
    perm = (j % DH) * H + j // DH
    x = f("x")[[0, 4, 1, 5, 2, 6, 3, 7]].transpose(2, 0, 1).reshape(P, B * T)

    feats = NF * P
    expert_of = np.minimum(np.arange(feats) // I, NE)

    def per_feature(shared, expert):
        v = np.concatenate([np.asarray(expert).reshape(E), np.asarray(shared).reshape(1), np.zeros(1, np.float32)])
        return v[expert_of].reshape(NF, P).T

    def features(a):
        v = np.concatenate([a.reshape(-1), np.zeros(feats - NE * I, np.float32)])
        return v.reshape(NF, P).T

    b1 = np.concatenate([f("L0_ffn_expert_b1"), f("L0_ffn_shared_b1")[None]])
    ea, sa = f("L0_ffn_expert_act"), f("L0_ffn_shared_act")
    params = [features(b1[:, 0::2]), features(b1[:, 1::2])] + [per_feature(sa[k], ea[:, k]) for k in range(5)]
    w1 = np.concatenate([f("L0_ffn_expert_w1"), f("L0_ffn_shared_w1")[None]])[:, perm, :]
    w1 = w1.transpose(1, 0, 2)
    pad = np.zeros((P, feats - NE * I), np.float32)
    w1 = np.concatenate([w1[:, :, 0::2].reshape(P, -1), pad, w1[:, :, 1::2].reshape(P, -1), pad], axis=1)
    w2 = np.concatenate([f("L0_ffn_expert_w2"), f("L0_ffn_shared_w2")[None]])[:, :, perm].reshape(NE * I, D)
    w2 = np.concatenate([w2, pad.T]).reshape(NF, P, D).transpose(1, 0, 2).reshape(P, NF * D)
    b2 = np.concatenate([f("L0_ffn_expert_b2"), f("L0_ffn_shared_b2")[None]])[:, perm]
    b2s = np.zeros((P, P), np.float32)
    b2s[0:NE] = b2
    b2s[32:32 + NE] = b2

    eye = np.eye(P, dtype=np.float32)
    zero16 = np.zeros((P, DH), np.float32)
    one16 = np.ones((P, DH), np.float32)
    mask8 = np.zeros((P, P), np.float32)
    mask8[j // DH, j] = 1.0
    maskp = np.stack([(j // DH) % 2 == 0, (j // DH) % 2 == 1], axis=1).astype(np.float32)
    hot = np.zeros((P, H), np.float32)
    hot[KR + np.arange(H), np.arange(H)] = 1.0
    parts = {
        "wtok": np.concatenate([f(n)[:, perm] for n in ("L0_tok_Wf", "L0_tok_Wi", "L0_tok_Wh")], axis=1),
        "btok": np.stack([f(n)[perm] for n in ("L0_tok_bf", "L0_tok_bi", "L0_tok_bh")], axis=1),
        "cmat": eye - np.float32(1.0 / P), "omat": np.full((P, P), 1.0 / P, np.float32),
        "wq": f("L0_attn_q_w")[:, perm].T, "wk": f("L0_attn_kv_w")[:D, perm].T, "wv": f("L0_attn_kv_w")[D:, perm].T,
        "ident": eye, "ones32": np.concatenate([one16, zero16, zero16, one16], axis=1), "mask8": mask8,
        "maskp": maskp, "hot": hot, "gate_w": f("L0_ffn_gate_w")[perm], "gate_b": np.repeat(f("L0_ffn_gate_b")[None], P, axis=0),
        "rank": np.repeat(np.arange(E, 0, -1, dtype=np.float32)[None], P, axis=0), "b2": b2s,
        "par": np.concatenate(params, axis=1),
    }
    consts = np.concatenate([parts[n] for n in CONSTS], axis=1)
    sel = np.zeros((P, NF, P), np.float32)
    for n in range(NE * I):
        sel[n // I, n // P, n % P] = 1.0
        sel[32 + n // I, n // P, n % P] = 1.0
    arrays = {"x": x, "consts": consts, "sel": sel.reshape(P, -1), "w1": w1, "w2": w2}
    return {k: np.ascontiguousarray(a) for k, a in arrays.items()}


def kernel(**inputs):
    import concourse.bacc as bacc
    from concourse.bass_utils import run_bass_kernel_spmd

    nc = bacc.Bacc("TRN2", target_bir_lowering=False, num_devices=1)
    arrays = {f"in_{k}": a for k, a in layout(inputs).items()}
    args = [nc.dram_tensor(k, a.shape, mybir.dt.from_np(a.dtype), kind="ExternalInput").ap() for k, a in arrays.items()]
    out = nc.dram_tensor("out", (B, N, D), F32, kind="ExternalOutput").ap()
    spill = nc.dram_tensor("spill", (UNITS, 4, P, 2, W), F32, kind="Internal").ap()
    build(nc, *args, spill, out)
    r = run_bass_kernel_spmd(nc, [arrays], core_ids=[0])
    return r.results[0]["out"]
```
